# Optimizing a Trainium2 kernel written in Bass

```python
import numpy as np
import jax
import jax.numpy as jnp

def _softmax(x, axis=-1):
    return jax.nn.softmax(x, axis=axis)

def _gelu(x):
    return jax.nn.gelu(x, approximate=True)

def _silu(x):
    return jax.nn.silu(x)

def _sigmoid(x):
    return jax.nn.sigmoid(x)

def _layernorm(x, axis=-1, eps=1e-05):
    m = jnp.mean(x, axis=axis, keepdims=True)
    v = jnp.var(x, axis=axis, keepdims=True)
    return (x - m) / jnp.sqrt(v + eps)

def _scatter_add(tgt, idx, src, axis=0):
    return tgt.at[idx].add(src)

def _segment_sum(src, seg, n):
    return jax.ops.segment_sum(src, seg, n)
kernel_name = 'mk_macaron_d1_jaxref_r4_eac462'

def setup_inputs(seed: int=0):
    np.random.seed(seed)
    _w = jnp.asarray

    def _L0_attn_setup():
        import jax, jax.numpy as jnp
        import numpy as np
        N_HEAD = 16
        LATENT = 32

        def _rotate_half(x):
            xe = x[..., ::2]
            xo = x[..., 1::2]
            return jnp.stack((-xo, xe), axis=-1).reshape(x.shape)

        def _rope_tables(T, latent_dim, dtype):
            inv_freq = 1.0 / 10000.0 ** (jnp.arange(0, latent_dim, 2, dtype=jnp.float32) / latent_dim)
            t = jnp.arange(T, dtype=jnp.float32)
            freqs = jnp.outer(t, inv_freq)
            cos = jnp.repeat(jnp.cos(freqs), 2, axis=-1)[:, :latent_dim]
            sin = jnp.repeat(jnp.sin(freqs), 2, axis=-1)[:, :latent_dim]
            return (cos.astype(dtype), sin.astype(dtype))
        key = jax.random.key(seed)
        ks = jax.random.split(key, 14)
        C = 256
        hd = C // N_HEAD
        L = LATENT
        s = 0.02
        return {'x': jax.random.normal(ks[0], (4, 512, C), jnp.float32), 'c_attn_w': jax.random.normal(ks[1], (3 * C, C), jnp.float32) * s, 'c_attn_b': jnp.zeros((3 * C,), jnp.float32), 'q2l_w': jax.random.normal(ks[2], (L, hd), jnp.float32) * s, 'q2l_b': jnp.zeros((L,), jnp.float32), 'kv2l_w': jax.random.normal(ks[3], (L, hd), jnp.float32) * s, 'kv2l_b': jnp.zeros((L,), jnp.float32), 'l2o_w': jax.random.normal(ks[4], (hd, L), jnp.float32) * s, 'l2o_b': jnp.zeros((hd,), jnp.float32), 'wqk_w': jax.random.normal(ks[5], (L, L), jnp.float32) * s, 'wqk_b': jnp.zeros((L,), jnp.float32), 'cproj_w': jax.random.normal(ks[6], (C, C), jnp.float32) * s, 'cproj_b': jnp.zeros((C,), jnp.float32)}
    _L0_attn_in = _L0_attn_setup()

    def _L0_ffn_setup():
        import jax, jax.numpy as jnp
        import numpy as np
        TOPK = 8
        NUM_EXPERTS = 64
        FFN = 768
        CAPACITY = 160

        def _swiglu(x, w1, w2):
            h = x @ w1.T
            x1, x2 = jnp.split(h, 2, axis=-1)
            return x1 * jax.nn.silu(x2) @ w2.T
        key = jax.random.key(seed)
        ks = jax.random.split(key, 6)
        B, S, H = (1, 128, 256)
        scale = 0.02
        return {'hidden_states': jax.random.normal(ks[0], (B, S, H), jnp.float32), 'wg': jax.random.normal(ks[1], (NUM_EXPERTS, H), jnp.float32) * scale, 'shared_w1': jax.random.normal(ks[2], (2 * FFN, H), jnp.float32) * scale, 'shared_w2': jax.random.normal(ks[3], (H, FFN), jnp.float32) * scale, 'expert_w1': jax.random.normal(ks[4], (NUM_EXPERTS, 2 * FFN, H), jnp.float32) * scale, 'expert_w2': jax.random.normal(ks[5], (NUM_EXPERTS, H, FFN), jnp.float32) * scale}
    _L0_ffn_in = _L0_ffn_setup()
    _d = {'L0_attn_x': _L0_attn_in['x'], 'L0_attn_c_attn_w': _L0_attn_in['c_attn_w'], 'L0_attn_c_attn_b': _L0_attn_in['c_attn_b'], 'L0_attn_q2l_w': _L0_attn_in['q2l_w'], 'L0_attn_q2l_b': _L0_attn_in['q2l_b'], 'L0_attn_kv2l_w': _L0_attn_in['kv2l_w'], 'L0_attn_kv2l_b': _L0_attn_in['kv2l_b'], 'L0_attn_l2o_w': _L0_attn_in['l2o_w'], 'L0_attn_l2o_b': _L0_attn_in['l2o_b'], 'L0_attn_wqk_w': _L0_attn_in['wqk_w'], 'L0_attn_wqk_b': _L0_attn_in['wqk_b'], 'L0_attn_cproj_w': _L0_attn_in['cproj_w'], 'L0_attn_cproj_b': _L0_attn_in['cproj_b'], 'L0_ffn_wg': _L0_ffn_in['wg'], 'L0_ffn_shared_w1': _L0_ffn_in['shared_w1'], 'L0_ffn_shared_w2': _L0_ffn_in['shared_w2'], 'L0_ffn_expert_w1': _L0_ffn_in['expert_w1'], 'L0_ffn_expert_w2': _L0_ffn_in['expert_w2']}
    _x0 = _d['L0_attn_x']
    _d['L0_attn_x'] = jax.random.normal(jax.random.fold_in(jax.random.key(seed), 1), (16, 512, 256), dtype=_x0.dtype)
    del _x0
    return _d

def reference(L0_attn_x, L0_attn_c_attn_w, L0_attn_c_attn_b, L0_attn_q2l_w, L0_attn_q2l_b, L0_attn_kv2l_w, L0_attn_kv2l_b, L0_attn_l2o_w, L0_attn_l2o_b, L0_attn_wqk_w, L0_attn_wqk_b, L0_attn_cproj_w, L0_attn_cproj_b, L0_ffn_wg, L0_ffn_shared_w1, L0_ffn_shared_w2, L0_ffn_expert_w1, L0_ffn_expert_w2):

    def _L0_attn_ref(x, c_attn_w, c_attn_b, q2l_w, q2l_b, kv2l_w, kv2l_b, l2o_w, l2o_b, wqk_w, wqk_b, cproj_w, cproj_b):
        import jax, jax.numpy as jnp
        import numpy as np
        N_HEAD = 16
        LATENT = 32

        def _rotate_half(x):
            xe = x[..., ::2]
            xo = x[..., 1::2]
            return jnp.stack((-xo, xe), axis=-1).reshape(x.shape)

        def _rope_tables(T, latent_dim, dtype):
            inv_freq = 1.0 / 10000.0 ** (jnp.arange(0, latent_dim, 2, dtype=jnp.float32) / latent_dim)
            t = jnp.arange(T, dtype=jnp.float32)
            freqs = jnp.outer(t, inv_freq)
            cos = jnp.repeat(jnp.cos(freqs), 2, axis=-1)[:, :latent_dim]
            sin = jnp.repeat(jnp.sin(freqs), 2, axis=-1)[:, :latent_dim]
            return (cos.astype(dtype), sin.astype(dtype))
        B, T, C = x.shape
        H = N_HEAD
        hd = C // H
        L = q2l_w.shape[0]
        qkv = x @ c_attn_w.T + c_attn_b
        q, k, v = jnp.split(qkv, 3, axis=2)

        def heads(t):
            return t.reshape(B, T, H, hd).transpose(0, 2, 1, 3)
        q, k, v = (heads(q), heads(k), heads(v))
        q_lat = q @ q2l_w.T + q2l_b
        k_lat = k @ kv2l_w.T + kv2l_b
        v_lat = v @ kv2l_w.T + kv2l_b
        cos, sin = _rope_tables(T, L, x.dtype)
        cos = cos[None, None]
        sin = sin[None, None]
        q_lat = q_lat * cos + _rotate_half(q_lat) * sin
        k_lat = k_lat * cos + _rotate_half(k_lat) * sin
        q_for_k = q_lat @ wqk_w.T + wqk_b
        att = jnp.einsum('bhql,bhkl->bhqk', q_for_k, k_lat) * L ** (-0.5)
        causal = jnp.tril(jnp.ones((T, T), dtype=bool))
        att = jnp.where(causal[None, None], att, -jnp.inf)
        att = jax.nn.softmax(att, axis=-1)
        y_lat = jnp.einsum('bhqk,bhkl->bhql', att, v_lat)
        y = y_lat @ l2o_w.T + l2o_b
        y = y.transpose(0, 2, 1, 3).reshape(B, T, C)
        return y @ cproj_w.T + cproj_b

    def _L0_ffn_ref(hidden_states, wg, shared_w1, shared_w2, expert_w1, expert_w2):
        import jax, jax.numpy as jnp
        import numpy as np
        TOPK = 8
        NUM_EXPERTS = 64
        FFN = 768
        CAPACITY = 160

        def _swiglu(x, w1, w2):
            h = x @ w1.T
            x1, x2 = jnp.split(h, 2, axis=-1)
            return x1 * jax.nn.silu(x2) @ w2.T
        B, S, H = hidden_states.shape
        T = B * S
        x = hidden_states.reshape(T, H)
        shared_out = _swiglu(x, shared_w1, shared_w2)
        logits = x.astype(jnp.float32) @ wg.T
        gates = jax.nn.softmax(logits, axis=-1)
        w_topk, idx_topk = jax.lax.top_k(gates, TOPK)
        denom = jnp.maximum(w_topk.sum(-1, keepdims=True), jnp.finfo(jnp.float32).eps)
        w_topk = w_topk / denom
        A = T * TOPK
        flat_e = idx_topk.reshape(A)
        flat_w = w_topk.reshape(A)
        flat_t = jnp.repeat(jnp.arange(T), TOPK)
        order = jnp.argsort(flat_e)
        se, st, sw = (flat_e[order], flat_t[order], flat_w[order])
        counts = jnp.zeros(NUM_EXPERTS, jnp.int32).at[flat_e].add(1)
        starts = jnp.cumsum(counts) - counts
        rank = jnp.arange(A) - starts[se]
        valid = rank < CAPACITY
        buf = jnp.zeros((NUM_EXPERTS, CAPACITY, H), x.dtype).at[se, rank].set(x[st], mode='drop')
        h = jnp.einsum('ech,efh->ecf', buf, expert_w1)
        x1, x2 = jnp.split(h, 2, axis=-1)
        out = jnp.einsum('ecf,ehf->ech', x1 * jax.nn.silu(x2), expert_w2)
        y = out[se, jnp.clip(rank, 0, CAPACITY - 1)]
        y = jnp.where(valid[:, None], y * sw[:, None].astype(y.dtype), 0.0)
        combined = jnp.zeros((T, H), x.dtype).at[st].add(y)
        return (shared_out + combined).reshape(B, S, H)
    x = L0_attn_x
    x = x + 0.5 * _L0_ffn_ref(_layernorm(x, axis=-1), L0_ffn_wg, L0_ffn_shared_w1, L0_ffn_shared_w2, L0_ffn_expert_w1, L0_ffn_expert_w2)
    x = x + _L0_attn_ref(_layernorm(x, axis=-1), L0_attn_c_attn_w, L0_attn_c_attn_b, L0_attn_q2l_w, L0_attn_q2l_b, L0_attn_kv2l_w, L0_attn_kv2l_b, L0_attn_l2o_w, L0_attn_l2o_b, L0_attn_wqk_w, L0_attn_wqk_b, L0_attn_cproj_w, L0_attn_cproj_b)
    x = x + 0.5 * _L0_ffn_ref(_layernorm(x, axis=-1), L0_ffn_wg, L0_ffn_shared_w1, L0_ffn_shared_w2, L0_ffn_expert_w1, L0_ffn_expert_w2)
    return x

_drawn_inputs = setup_inputs


def setup_inputs(seed=0):
    import zlib

    import numpy as np

    out = dict(_drawn_inputs(seed))
    spreads = {'L0_attn_c_attn_b': (0.0, 0.8),
     'L0_attn_q2l_b': (0.0, 0.8),
     'L0_attn_kv2l_b': (0.0, 0.8),
     'L0_attn_l2o_b': (0.0, 0.1),
     'L0_attn_wqk_b': (0.0, 0.8),
     'L0_attn_cproj_b': (0.0, 0.1)}
    factors = {'L0_attn_c_attn_w': 8.0,
     'L0_attn_q2l_w': 8.0,
     'L0_attn_kv2l_w': 8.0,
     'L0_attn_l2o_w': 8.0,
     'L0_attn_wqk_w': 8.0,
     'L0_ffn_wg': 8.0,
     'L0_ffn_expert_w1': 8.0,
     'L0_ffn_expert_w2': 8.0}
    for name, (base, spread) in spreads.items():
        noise = np.random.default_rng([zlib.crc32(name.encode()), seed]).standard_normal(out[name].shape)
        drawn = base * np.exp(spread * noise) if base else spread * noise
        out[name] = jnp.asarray(drawn.astype(out[name].dtype))
    for name, factor in factors.items():
        out[name] = (out[name] * factor).astype(out[name].dtype)
    return out
```

```python
from contextlib import ExitStack

import numpy as np

import concourse.bass as bass
from concourse import mybir

ALU = mybir.AluOpType
ACT = mybir.ActivationFunctionType
AX = mybir.AxisListType
F32 = mybir.dt.float32
BF16 = mybir.dt.bfloat16
I32 = mybir.dt.int32

P = 128
BATCH, SEQ, C = 16, 512, 256
TOK = BATCH * SEQ
CC = C // P
E, TOPK, CAP, F = 64, 8, 160, 768
FC = F // P
BLK = 512
TPB = BLK // P
NBLK = TOK // BLK
NT = TOK // P
ROW = C + E
GRP = 4
NG = E // GRP
TAIL = CAP - P
NH, HD, L = 16, 16, 32
EPS = 1e-5
FLT_EPS = float(np.finfo(np.float32).eps)


def need(eng, sem, value):
    if isinstance(value, int) and value <= 0:
        return
    eng.wait_ge(sem, value)


class Steps:

    def __init__(self, eng, sem):
        self.eng, self.sem, self.base, self.n = eng, sem, 0, 0

    def step(self, instruction):
        instruction.then_inc(self.sem, 1)
        self.n += 1

    def settle(self):
        need(self.eng, self.sem, self.base + self.n)

    def settle_on(self, cell):
        self.settle()
        self.eng.memset(cell, 0.0)

    def loop(self, turn, per_turn):
        self.base, self.entry, self.n = self.base + self.n + turn * per_turn, self.n + self.base, 0
        self.per_turn = per_turn

    def end_loop(self, turns):
        assert self.n == self.per_turn, (self.n, self.per_turn)
        self.base, self.n = self.entry + turns * self.per_turn, 0


def rsqrt_refined(dve, st, out, var, std, tmp):
    for step in (lambda: dve.reciprocal(out[:], std[:]),
                 lambda: dve.tensor_tensor(tmp[:], out[:], out[:], ALU.mult),
                 lambda: dve.tensor_tensor(tmp[:], tmp[:], var[:], ALU.mult),
                 lambda: dve.tensor_scalar(tmp[:], tmp[:], -0.5, 1.5, ALU.mult, ALU.add),
                 lambda: dve.tensor_tensor(out[:], out[:], tmp[:], ALU.mult)):
        st.step(step())
        st.settle()


class Blk:

    def __init__(self, pair, odd):
        self.pair, self.odd = pair + odd // 2, odd % 2
        self.i = self.pair * 2 + self.odd

    def plus(self, k):
        return Blk(self.pair, self.odd + k)


def pairs_loop(nc, eng, n_blocks, body, steps=None):
    body(Blk(0, 0), 2)
    start = steps.n if steps else 0
    body(Blk(0, 1), 2)
    per = 2 * (steps.n - start) if steps else 0
    turns = n_blocks // 2 - 2
    with eng.Fori(1, 1 + turns) as pair:
        if steps:
            steps.loop(pair - 1, per)
        body(Blk(pair, 0), 2)
        body(Blk(pair, 1), 2)
    if steps:
        steps.end_loop(turns)
    body(Blk(n_blocks // 2 - 1, 0), 1)
    body(Blk(n_blocks // 2 - 1, 1), 0)


def token_major(dram, i):
    return dram[bass.ds(i * BLK, BLK), :].rearrange("(t p) n -> p t n", p=P)


def ffn_dense(nc, tag, src, acc, xtab, cumtab, cend_dram, a):
    with ExitStack() as ctx:
        def sb(name, shape, dt=F32):
            return ctx.enter_context(nc.sbuf_tensor(f"{tag}_{name}", shape, dt))

        def sem(name):
            return nc.alloc_semaphore(f"{tag}_{name}")

        ident = sb("ident", [P, P])
        tri_f = sb("tri_f", [P, TPB, BLK])
        tri = sb("tri", [P, TPB, BLK], BF16)
        wg_sb = sb("wg", [P, CC, E])
        w1 = sb("w1", [P, CC, 2 * F])
        w2 = sb("w2", [P, FC, C])
        xin = [sb(f"xin{b}", [P, TPB, C]) for b in range(2)]
        xres = [sb(f"xres{b}", [P, TPB, C]) for b in range(2)]
        xln = [sb(f"xln{b}", [P, TPB, C]) for b in range(2)]
        xT = [sb(f"xT{b}", [P, CC, BLK]) for b in range(2)]
        hT = [sb(f"hT{b}", [P, FC, BLK]) for b in range(2)]
        silu = [sb(f"silu{b}", [P, BLK]) for b in range(2)]
        xout = [sb(f"xout{b}", [P, TPB, C]) for b in range(2)]
        gates_out = [sb(f"gates_out{b}", [P, TPB, E]) for b in range(2)]
        cum_sb = [sb(f"cum{b}", [E, BLK]) for b in range(2)]
        carry = sb("carry", [E, 1])
        cend = sb("cend", [E, NT])
        stats = sb("stats", [P, TPB, 6])
        mv = sb("mv", [P, TPB, 2])
        varp = sb("varp", [P, TPB])
        std = sb("std", [P, TPB])
        rstd = sb("rstd", [P, TPB])
        newton = sb("newton", [P, TPB])
        negmax = sb("negmax", [P, TPB])
        zlog = sb("zlog", [P, TPB, E])
        ez = sb("ez", [P, TPB, E])
        gate = sb("gate", [P, TPB, E])
        struck = sb("struck", [P, TPB, E])
        gscaled = sb("gscaled", [P, TPB, E])
        mask = sb("mask", [P, TPB, E], BF16)
        top8 = sb("top8", [P, TPB, TOPK])
        esum = sb("esum", [P, TPB])
        rsum = sb("rsum", [P, TPB])
        tsum = sb("tsum", [P, TPB])
        tclip = sb("tclip", [P, TPB])
        trec = sb("trec", [P, TPB])
        thalf = sb("thalf", [P, TPB])
        unused = sb("unused", [P, 1])
        zrow = sb("zrow", [P, ROW])
        brow = sb("brow", [E, P])

        def bank(name):
            return ctx.enter_context(nc.psum_tensor(f"{tag}_{name}", [P, 512], F32))

        side = [bank(f"side{c}") for c in range(2)]
        up1 = [bank(f"up1_{b}") for b in range(2)]
        up2 = [bank(f"up2_{b}") for b in range(2)]
        down = [bank(f"down{b}") for b in range(2)]

        const_in = sem("const_in")
        x_in = [sem(f"x_in{b}") for b in range(2)]
        xres_in = [sem(f"xres_in{b}") for b in range(2)]
        xln_kept = [sem(f"xln_kept{b}") for b in range(2)]
        gates_kept = [sem(f"gates_kept{b}") for b in range(2)]
        cum_kept = [sem(f"cum_kept{b}") for b in range(2)]
        out_kept = [sem(f"out_kept{b}") for b in range(2)]
        pad_kept = sem("pad_kept")
        pads_set = sem("pads_set")
        vec = sem("vec")
        tri_ready = sem("tri_ready")
        var_ready = sem("var_ready")
        std_ready = sem("std_ready")
        ln_ready = sem("ln_ready")
        turned = sem("turned")
        xT_ready = sem("xT_ready")
        logits_ready = sem("logits_ready")
        logits_read = sem("logits_read")
        ez_ready = sem("ez_ready")
        route_ready = sem("route_ready")
        cum_ready = sem("cum_ready")
        cum_read = sem("cum_read")
        up_ready = sem("up_ready")
        silu_ready = sem("silu_ready")
        h_ready = sem("h_ready")
        down_ready = sem("down_ready")
        out_ready = sem("out_ready")
        N_CONST = 5

        with nc.Block() as block:

            @block.sync
            def _(sp):
                for dst, s in ((ident, a["ident"]), (wg_sb, a["wg"]), (w1, a["sw1"]), (w2, a["sw2"]),
                               (tri_f, a["tri"])):
                    sp.dma_start(dst[:], s).then_inc(const_in, 16)

                def load_x(b):
                    need(sp, ln_ready, b.i - 1)
                    sp.dma_start(xin[b.odd][:], token_major(src, b.i)).then_inc(x_in[b.odd], 16)

                load_x(Blk(0, 0))
                load_x(Blk(0, 1))
                sp.wait_ge(pads_set, 2)
                sp.dma_start(xtab[TOK:TOK + P, :], zrow[:]).then_inc(pad_kept, 16)
                sp.dma_start(acc[TOK:TOK + P, :], zrow[:, 0:C]).then_inc(pad_kept, 16)
                sp.dma_start(cumtab[NT * E:(NT + 1) * E, :], brow[:]).then_inc(pad_kept, 16)

                def keep_xln(b):
                    sp.wait_ge(ln_ready, b.i + 1)
                    sp.dma_start(token_major(xtab, b.i)[:, :, 0:C], xln[b.odd][:]).then_inc(xln_kept[b.odd], 16)

                def keep_route(b):
                    sp.wait_ge(route_ready, b.i + 1)
                    sp.dma_start(token_major(xtab, b.i)[:, :, C:ROW], gates_out[b.odd][:]).then_inc(gates_kept[b.odd], 16)
                    sp.wait_ge(cum_read, b.i + 1)
                    sp.dma_start(cumtab[bass.ds(b.i * (TPB * E), TPB * E), :].rearrange("(t e) n -> e t n", e=E),
                                 cum_sb[b.odd][:].rearrange("e (t n) -> e t n", n=P)).then_inc(cum_kept[b.odd], 16)

                keep_xln(Blk(0, 0))
                keep_xln(Blk(0, 1))
                keep_route(Blk(0, 0))

                def turn(b, more):
                    need(sp, out_ready, 2 * (b.i - 1))
                    sp.dma_start(xres[b.odd][:], token_major(src, b.i)).then_inc(xres_in[b.odd], 16)
                    if more >= 2:
                        load_x(b.plus(2))
                        keep_xln(b.plus(2))
                    if more >= 1:
                        keep_route(b.plus(1))
                    sp.wait_ge(out_ready, 2 * b.i + 2)
                    sp.dma_start(token_major(acc, b.i), xout[b.odd][:]).then_inc(out_kept[b.odd], 16)

                pairs_loop(nc, sp, NBLK, turn)
                sp.dma_start(cend_dram, cend[:]).then_inc(pad_kept, 16)
                sp.wait_ge(pad_kept, 16 * 4)
                for kept in xln_kept + gates_kept + cum_kept + out_kept:
                    sp.wait_ge(kept, 16 * (NBLK // 2))

            @block.gpsimd
            def _(pool):
                nc.gpsimd.memset(zrow[:], 0.0).then_inc(pads_set, 1)
                nc.gpsimd.memset(brow[:], 1.0e9).then_inc(pads_set, 1)

            @block.tensor
            def _(pe):
                def turn_x(b):
                    pe.wait_ge(ln_ready, b.i + 1)
                    need(pe, logits_read, b.i)
                    need(pe, cum_read, b.i)
                    for c in range(CC):
                        for t in range(TPB):
                            last = pe.transpose(side[c][:, t * P:(t + 1) * P],
                                                xln[b.odd][:, t, c * P:(c + 1) * P], ident[:])
                    last.then_inc(turned, 1)

                def logits(b):
                    pe.wait_ge(xT_ready, b.i + 1)
                    for t in range(TPB):
                        for c in range(CC):
                            last = pe.matmul(side[0][:, t * E:(t + 1) * E], xT[b.odd][:, c, t * P:(t + 1) * P],
                                             wg_sb[:, c, :], start=(c == 0), stop=(c == CC - 1))
                    last.then_inc(logits_ready, 1)

                def ranks(b):
                    pe.wait_ge(route_ready, b.i + 1)
                    for t in range(TPB):
                        last = pe.matmul(side[1][0:E, t * P:BLK], mask[:, t, :], tri[:, t, t * P:BLK],
                                         start=(t == 0), stop=(t == TPB - 1), skip_group_check=True)
                    last.then_inc(cum_ready, 1)

                def up(b, f):
                    need(pe, h_ready, b.i * FC + f - 1)
                    for half, dst in ((0, up1[f % 2]), (1, up2[f % 2])):
                        for c in range(CC):
                            o = half * F + f * P
                            last = pe.matmul(dst[:], w1[:, c, o:o + P], xT[b.odd][:, c, :],
                                             start=(c == 0), stop=(c == CC - 1))
                    last.then_inc(up_ready, 1)

                def downs(b):
                    for q in range(2):
                        need(pe, out_ready, 2 * b.i + q - 1)
                        for t in range(2 * q, 2 * q + 2):
                            for f in range(FC):
                                pe_ready = b.i * FC + f + 1
                                if t == 0:
                                    pe.wait_ge(h_ready, pe_ready)
                                last = pe.matmul(down[q][:, (t % 2) * C:(t % 2 + 1) * C],
                                                 hT[b.odd][:, f, t * P:(t + 1) * P], w2[:, f, :],
                                                 start=(f == 0), stop=(f == FC - 1))
                        last.then_inc(down_ready, 1)

                pe.wait_ge(const_in, 16 * N_CONST)
                pe.wait_ge(tri_ready, 1)
                turn_x(Blk(0, 0))
                logits(Blk(0, 0))
                ranks(Blk(0, 0))

                def turn(b, more):
                    if more:
                        turn_x(b.plus(1))
                    up(b, 0)
                    if more:
                        logits(b.plus(1))
                    for f in range(1, FC):
                        up(b, f)
                    if more:
                        ranks(b.plus(1))
                    downs(b)

                pairs_loop(nc, pe, NBLK, turn)

            @block.scalar
            def _(act):
                def std_of(b):
                    act.wait_ge(var_ready, b.i + 1)
                    act.activation(std[:], varp[:], ACT.Sqrt).then_inc(std_ready, 1)

                def out_xT(b):
                    act.wait_ge(turned, b.i + 1)
                    act.activation(xT[b.odd][:, 0, :], side[0][:], ACT.Copy)
                    act.activation(xT[b.odd][:, 1, :], side[1][:], ACT.Copy).then_inc(xT_ready, 1)

                def exps(b):
                    act.wait_ge(logits_read, b.i + 1)
                    act.activation(ez[:], zlog[:], ACT.Exp).then_inc(ez_ready, 1)

                def silus(b, f):
                    act.wait_ge(up_ready, b.i * FC + f + 1)
                    need(act, h_ready, b.i * FC + f - 1)
                    act.activation(silu[f % 2][:], up2[f % 2][:], ACT.Silu).then_inc(silu_ready, 1)

                std_of(Blk(0, 0))
                std_of(Blk(0, 1))
                out_xT(Blk(0, 0))
                exps(Blk(0, 0))

                def turn(b, more):
                    if more:
                        out_xT(b.plus(1))
                    silus(b, 0)
                    silus(b, 1)
                    if more:
                        exps(b.plus(1))
                    if more >= 2:
                        std_of(b.plus(2))
                    for f in range(2, FC):
                        silus(b, f)

                pairs_loop(nc, act, NBLK, turn)

            @block.vector
            def _(dve):
                st = Steps(dve, vec)
                dve.wait_ge(const_in, 16 * N_CONST)
                dve.tensor_copy(tri[:], tri_f[:]).then_inc(tri_ready, 1)
                st.step(dve.memset(carry[:], 0.0))

                def ln_stats(b):
                    dve.wait_ge(x_in[b.odd], 16 * (b.pair + 1))
                    for t in range(TPB):
                        st.step(dve.bn_stats(stats[:, t, :], xin[b.odd][:, t, :]))
                    st.settle_on(unused[:])
                    for t in range(TPB):
                        st.step(dve.bn_aggr(mv[:, t, :], stats[:, t, :]))
                    st.settle()
                    need(dve, std_ready, b.i)
                    dve.tensor_scalar(varp[:], mv[:, :, 1], EPS, None, ALU.add).then_inc(var_ready, 1)

                def ln_apply(b):
                    dve.wait_ge(std_ready, b.i + 1)
                    rsqrt_refined(dve, st, rstd, varp, std, newton)
                    need(dve, xln_kept[b.odd], 16 * b.pair)
                    need(dve, turned, b.i - 1)
                    for t in range(TPB):
                        last = dve.tensor_scalar(xln[b.odd][:, t, :], xin[b.odd][:, t, :], mv[:, t, 0:1],
                                                 rstd[:, t:t + 1], ALU.subtract, ALU.mult)
                        if t < TPB - 1:
                            st.step(last)
                    last.then_inc(ln_ready, 1)

                def bc(x, n):
                    return x.unsqueeze(2).to_broadcast([P, TPB, n])

                def route_a(b):
                    lg = side[0][:, 0:TPB * E].rearrange("p (t e) -> p t e", t=TPB)
                    dve.wait_ge(logits_ready, b.i + 1)
                    st.step(dve.tensor_reduce(negmax[:], lg, AX.X, ALU.max, negate=True))
                    st.settle()
                    dve.tensor_tensor(zlog[:], lg, bc(negmax[:], E), ALU.add).then_inc(logits_read, 1)

                def route_b(b):
                    dve.wait_ge(ez_ready, b.i + 1)
                    st.step(dve.tensor_reduce(esum[:], ez[:], AX.X, ALU.add))
                    st.settle()
                    st.step(dve.reciprocal(rsum[:], esum[:]))
                    st.settle()
                    st.step(dve.tensor_tensor(gate[:], ez[:], bc(rsum[:], E), ALU.mult))
                    st.settle_on(unused[:])
                    for t in range(TPB):
                        st.step(dve.max(top8[:, t, :], gate[:, t, :]))
                    st.settle()

                def route_c(b):
                    for t in range(TPB):
                        st.step(dve.match_replace(struck[:, t, :], top8[:, t, :], gate[:, t, :], -1.0))
                    st.step(dve.tensor_reduce(tsum[:], top8[:], AX.X, ALU.add))
                    st.settle()
                    need(dve, cum_ready, b.i)
                    st.step(dve.tensor_scalar(mask[:], struck[:], 0.0, None, ALU.is_lt))
                    st.step(dve.tensor_scalar(tclip[:], tsum[:], FLT_EPS, None, ALU.max))
                    st.settle()
                    st.step(dve.reciprocal(trec[:], tclip[:]))
                    st.settle()
                    st.step(dve.tensor_scalar(thalf[:], trec[:], 0.5, None, ALU.mult))
                    st.settle()
                    st.step(dve.tensor_tensor(gscaled[:], gate[:], bc(thalf[:], E), ALU.mult))
                    st.settle()
                    need(dve, gates_kept[b.odd], 16 * b.pair)
                    dve.tensor_tensor(gates_out[b.odd][:], gscaled[:], mask[:], ALU.mult).then_inc(route_ready, 1)

                def cum_out(b):
                    dve.wait_ge(cum_ready, b.i + 1)
                    need(dve, cum_kept[b.odd], 16 * b.pair)
                    st.settle()
                    st.step(dve.tensor_scalar(cum_sb[b.odd][:], side[1][0:E, :], carry[:], None, ALU.add))
                    st.settle()
                    st.step(dve.tensor_copy(carry[:], cum_sb[b.odd][:, BLK - 1:BLK]))
                    dve.tensor_copy(cend[:, bass.ds(b.i * TPB, TPB)],
                                    cum_sb[b.odd][:, P - 1:BLK:P]).then_inc(cum_read, 1)

                def product(b, f):
                    dve.wait_ge(silu_ready, b.i * FC + f + 1)
                    need(dve, down_ready, 2 * (b.i - 1))
                    dve.tensor_tensor(hT[b.odd][:, f, :], up1[f % 2][:], silu[f % 2][:], ALU.mult)\
                       .then_inc(h_ready, 1)

                def out_sum(b):
                    dve.wait_ge(xres_in[b.odd], 16 * (b.pair + 1))
                    need(dve, out_kept[b.odd], 16 * b.pair)
                    for q in range(2):
                        dve.wait_ge(down_ready, 2 * b.i + q + 1)
                        dve.scalar_tensor_tensor(xout[b.odd][:, 2 * q:2 * q + 2, :],
                                                 down[q][:].rearrange("p (t n) -> p t n", t=2), 0.5,
                                                 xres[b.odd][:, 2 * q:2 * q + 2, :], ALU.mult, ALU.add)\
                           .then_inc(out_ready, 1)

                ln_stats(Blk(0, 0))
                ln_apply(Blk(0, 0))
                ln_stats(Blk(0, 1))
                ln_apply(Blk(0, 1))
                route_a(Blk(0, 0))
                route_b(Blk(0, 0))
                route_c(Blk(0, 0))
                cum_out(Blk(0, 0))

                def turn(b, more):
                    if more >= 2:
                        ln_stats(b.plus(2))
                    product(b, 0)
                    if more:
                        route_a(b.plus(1))
                    product(b, 1)
                    if more:
                        route_b(b.plus(1))
                    product(b, 2)
                    if more:
                        route_c(b.plus(1))
                    product(b, 3)
                    product(b, 4)
                    if more >= 2:
                        ln_apply(b.plus(2))
                    product(b, 5)
                    if more:
                        cum_out(b.plus(1))
                    out_sum(b)

                pairs_loop(nc, dve, NBLK, turn, st)


def ffn_routed(nc, tag, acc, xtab, cumtab, cend_dram, a):
    WE = CC * 2 * F + FC * C
    HF = FC // 2
    CH = GRP + 1
    with ExitStack() as ctx:
        def sb(name, shape, dt=F32):
            return ctx.enter_context(nc.sbuf_tensor(f"{tag}_{name}", shape, dt))

        def sem(name):
            return nc.alloc_semaphore(f"{tag}_{name}")

        def bank(name):
            return ctx.enter_context(nc.psum_tensor(f"{tag}_{name}", [P, 512], F32))

        ident = sb("ident", [P, P])
        slot = sb("slot", [P, CH + 1])
        erow = sb("erow", [P, NG, CH])
        cend_all = sb("cend_all", [P, E, NT])
        cend_tail = sb("cend_tail", [P, NG, NT])
        w = [sb(f"w{k}", [P, WE]) for k in range(GRP)]
        w1 = [x[:, 0:CC * 2 * F].rearrange("p (c f) -> p c f", c=CC) for x in w]
        w2 = [x[:, CC * 2 * F:WE].rearrange("p (f n) -> p f n", f=FC) for x in w]
        unused = sb("unused", [P, 3])
        ended = sb("ended", [P, CH, NT])
        tile_of = sb("tile_of", [P, CH])
        cum_idx = sb("cum_idx", [P, CH], I32)
        cum_rows = sb("cum_rows", [P, CH, P])
        below = sb("below", [P, CH, P])
        count = sb("count", [P, CH])
        token0 = sb("token0", [P, CH])
        pad = sb("pad", [P, CH])
        token = sb("token", [P, CH])
        x_idx = sb("x_idx", [P, CH], I32)
        y_idx = sb("y_idx", [P, GRP], I32)
        yt_idx = sb("yt_idx", [TAIL, GRP], I32)
        x_rows = sb("x_rows", [P, CH, ROW])
        xT = sb("xT", [P, CC, GRP, CAP])
        wy = sb("wy", [P, GRP])
        wyt = sb("wyt", [TAIL, GRP])
        silu = [sb(f"silu{b}", [P, HF * CAP]) for b in range(2)]
        hT = [sb(f"hT{b}", [P, FC, CAP]) for b in range(2)]
        yT = sb("yT", [P, CC, CAP])
        y = sb("y", [P, GRP, C])
        yt = sb("yt", [TAIL, GRP, C])

        up1 = [bank(f"up1_{b}") for b in range(2)]
        up2 = [bank(f"up2_{b}") for b in range(2)]
        down = bank("down")
        back = bank("back")
        turn_x = [bank(f"turn{c}") for c in range(CC)]

        const_in = sem("const_in")
        w_in = [sem(f"w_in{k}") for k in range(GRP)]
        vec = sem("vec")
        unused_set = sem("unused_set")
        held = sem("held")
        cum_idx_ready = sem("cum_idx_ready")
        cum_in = sem("cum_in")
        token_ready = sem("token_ready")
        x_idx_ready = sem("x_idx_ready")
        y_idx_ready = sem("y_idx_ready")
        x_rows_in = sem("x_rows_in")
        turned = sem("turned")
        xT_ready = sem("xT_ready")
        wy_ready = sem("wy_ready")
        up_ready = sem("up_ready")
        silu_ready = sem("silu_ready")
        h_ready = sem("h_ready")
        down_ready = sem("down_ready")
        yT_ready = sem("yT_ready")
        back_ready = sem("back_ready")
        y_ready = sem("y_ready")
        y_added = sem("y_added")
        N_CONST = 4 + GRP

        def groups_loop(eng, body, steps=None):
            start = steps.n if steps else 0
            body(0, 2)
            per = steps.n - start if steps else 0
            with eng.Fori(1, NG - 2) as g:
                if steps:
                    steps.loop(g - 1, per)
                body(g, 2)
            if steps:
                steps.end_loop(NG - 3)
            body(NG - 2, 1)
            body(NG - 1, 0)

        with nc.Block() as block:

            @block.sync
            def _(sp):
                sp.dma_start(ident[:], a["ident"]).then_inc(const_in, 16)
                sp.dma_start(slot[:], a["slot"]).then_inc(const_in, 16)
                sp.dma_start(erow[:], a["erow"]).then_inc(const_in, 16)
                sp.dma_start(cend_all[:], cend_dram.unsqueeze(0).to_broadcast([P, E, NT])).then_inc(const_in, 16)
                for k in range(GRP):
                    rows = cend_dram.rearrange("(g k) t -> k g t", k=GRP)[k].unsqueeze(0)
                    sp.dma_start(cend_tail[TAIL * k:TAIL * (k + 1), :, :],
                                 rows.to_broadcast([TAIL, NG, NT])).then_inc(const_in, 16)

                def turn(g, more):
                    for k in range(GRP):
                        need(sp, down_ready, GRP * (g - 1) + k + 1)
                        sp.dma_start(w[k][:], a["experts"][bass.ds(g * GRP + k, 1), :, :].squeeze(0))\
                          .then_inc(w_in[k], 16)

                groups_loop(sp, turn)

            @block.gpsimd
            def _(pool):
                st = Steps(pool, held)

                def settle():
                    st.settle()
                    st.step(pool.tensor_tensor(unused[:, 0:1], unused[:, 1:2], unused[:, 2:3], ALU.add))

                pool.memset(unused[:], 0.0).then_inc(unused_set, 1)
                pool.wait_ge(unused_set, 1)

                def gather_cum(g):
                    pool.wait_ge(cum_idx_ready, g + 1)
                    need(pool, token_ready, g)
                    settle()
                    for j in range(CH):
                        pool.indirect_dma_start(cum_rows[:, j, :], None, cumtab,
                                                bass.IndirectOffsetOnAxis(ap=cum_idx[:, j:j + 1], axis=0))\
                            .then_inc(cum_in, 16)

                def gather_x(g):
                    pool.wait_ge(x_idx_ready, g + 1)
                    need(pool, turned, 2 * g)
                    need(pool, wy_ready, g)
                    settle()
                    for j in range(CH):
                        pool.indirect_dma_start(x_rows[:, j, :], None, xtab,
                                                bass.IndirectOffsetOnAxis(ap=x_idx[:, j:j + 1], axis=0))\
                            .then_inc(x_rows_in, 16)

                def add_y(g, k):
                    pool.wait_ge(y_ready, g * GRP + k + 1)
                    if k == 0:
                        pool.wait_ge(y_idx_ready, g + 1)
                    need(pool, y_added, 32 * (g * GRP + k))
                    settle()
                    for idx, rows in ((y_idx, y), (yt_idx, yt)):
                        pool.indirect_dma_start(acc, bass.IndirectOffsetOnAxis(ap=idx[:, k:k + 1], axis=0),
                                                rows[:, k, :], None, compute_op=ALU.add).then_inc(y_added, 16)

                gather_cum(0)
                gather_cum(1)
                gather_x(0)

                def turn(g, more):
                    if more >= 1:
                        gather_x(g + 1)
                    if more >= 2:
                        gather_cum(g + 2)
                    for k in range(GRP):
                        add_y(g, k)

                groups_loop(pool, turn, st)
                pool.wait_ge(y_added, 32 * E)

            @block.tensor
            def _(pe):
                def turn_full(g):
                    pe.wait_ge(x_rows_in, 16 * CH * (g + 1))
                    need(pe, xT_ready, 2 * g)
                    for c in range(CC):
                        for k in range(GRP):
                            last = pe.transpose(turn_x[c][:, k * P:(k + 1) * P],
                                                x_rows[:, k, c * P:(c + 1) * P], ident[:])
                    last.then_inc(turned, 1)

                def turn_tail(g):
                    pe.wait_ge(xT_ready, 2 * g + 1)
                    for c in range(CC):
                        last = pe.transpose(turn_x[0][:, c * P:(c + 1) * P],
                                            x_rows[:, GRP, c * P:(c + 1) * P], ident[:])
                    last.then_inc(turned, 1)

                def up(g, k, s):
                    x = g * GRP + k
                    if s == 0:
                        pe.wait_ge(w_in[k], 16 * (g + 1))
                        if k == 0:
                            pe.wait_ge(xT_ready, 2 * g + 2)
                    need(pe, h_ready, 2 * x + s - 1)
                    for half, dst in ((0, up1[s]), (1, up2[s])):
                        for j in range(HF):
                            o = half * F + (s * HF + j) * P
                            for c in range(CC):
                                last = pe.matmul(dst[:, j * CAP:(j + 1) * CAP], w1[k][:, c, o:o + P],
                                                 xT[:, c, k, :], start=(c == 0), stop=(c == CC - 1))
                    last.then_inc(up_ready, 1)

                def downs(g, k):
                    x = g * GRP + k
                    need(pe, yT_ready, x)
                    pe.wait_ge(h_ready, 2 * x + 2)
                    for c in range(CC):
                        for f in range(FC):
                            last = pe.matmul(down[:, c * CAP:(c + 1) * CAP], w2[k][:, f, c * P:(c + 1) * P],
                                             hT[k % 2][:, f, :], start=(f == 0), stop=(f == FC - 1))
                    last.then_inc(down_ready, 1)

                def backs(g, k):
                    x = g * GRP + k
                    pe.wait_ge(yT_ready, x + 1)
                    need(pe, y_ready, x)
                    for c in range(CC):
                        pe.transpose(back[:, c * P:(c + 1) * P], yT[:, c, 0:P], ident[:])
                        last = pe.transpose(back[0:TAIL, C + c * P:C + (c + 1) * P], yT[:, c, P:CAP], ident[:])
                    last.then_inc(back_ready, 1)

                pe.wait_ge(const_in, 16 * N_CONST)
                turn_full(0)
                turn_tail(0)

                def turn(g, more):
                    up(g, 0, 0)
                    up(g, 0, 1)
                    for k in range(1, GRP):
                        up(g, k, 0)
                        downs(g, k - 1)
                        up(g, k, 1)
                        backs(g, k - 1)
                    if more:
                        turn_full(g + 1)
                    downs(g, GRP - 1)
                    if more:
                        turn_tail(g + 1)
                    backs(g, GRP - 1)

                groups_loop(pe, turn)

            @block.scalar
            def _(act):
                def out_xT(g):
                    act.wait_ge(turned, 2 * g + 1)
                    for c in range(CC):
                        last = act.activation(xT[:, c, :, 0:P], turn_x[c][:].rearrange("p (k n) -> p k n", k=GRP),
                                              ACT.Copy)
                    last.then_inc(xT_ready, 1)

                def out_xT_tail(g):
                    act.wait_ge(turned, 2 * g + 2)
                    for c in range(CC):
                        last = act.activation(xT[:, c, :, P:CAP],
                                              turn_x[0][:, c * P:(c + 1) * P].rearrange("p (k n) -> p k n", k=GRP),
                                              ACT.Copy)
                    last.then_inc(xT_ready, 1)

                def silus(g, k, s):
                    x = g * GRP + k
                    act.wait_ge(up_ready, 2 * x + s + 1)
                    need(act, h_ready, 2 * x + s - 1)
                    act.activation(silu[s][:], up2[s][:, 0:HF * CAP], ACT.Silu).then_inc(silu_ready, 1)

                def out_yT(g, k):
                    x = g * GRP + k
                    act.wait_ge(down_ready, x + 1)
                    need(act, back_ready, x)
                    act.activation(yT[:], down[:, 0:CC * CAP].rearrange("p (c n) -> p c n", c=CC), ACT.Copy)\
                       .then_inc(yT_ready, 1)

                out_xT(0)
                out_xT_tail(0)

                def turn(g, more):
                    silus(g, 0, 0)
                    silus(g, 0, 1)
                    for k in range(1, GRP):
                        silus(g, k, 0)
                        out_yT(g, k - 1)
                        silus(g, k, 1)
                    if more:
                        out_xT(g + 1)
                    out_yT(g, GRP - 1)
                    if more:
                        out_xT_tail(g + 1)

                groups_loop(act, turn)

            @block.vector
            def _(dve):
                st = Steps(dve, vec)

                def tiles_of(g):
                    need(dve, token_ready, g)
                    st.step(dve.tensor_scalar(ended[:, 0:GRP, :], cend_all[:, bass.ds(g * GRP, GRP), :],
                                              slot[:, 0:1], None, ALU.is_le))
                    st.step(dve.tensor_scalar(ended[:, GRP, :], cend_tail[:, bass.ds(g, 1), :].rearrange("p a t -> p (a t)"),
                                              slot[:, GRP:GRP + 1], None, ALU.is_le))
                    st.settle()
                    st.step(dve.tensor_reduce(tile_of[:], ended[:], AX.X, ALU.add))
                    st.settle()
                    need(dve, cum_in, 16 * CH * g)
                    dve.scalar_tensor_tensor(cum_idx[:], tile_of[:], float(E),
                                             erow[:, bass.ds(g, 1), :].rearrange("p a j -> p (a j)"),
                                             ALU.mult, ALU.add).then_inc(cum_idx_ready, 1)

                def tokens_of(g):
                    dve.wait_ge(cum_in, 16 * CH * (g + 1))
                    st.step(dve.tensor_tensor(below[:], cum_rows[:],
                                              slot[:, 0:CH].unsqueeze(2).to_broadcast([P, CH, P]), ALU.is_le))
                    st.settle()
                    st.step(dve.tensor_reduce(count[:], below[:], AX.X, ALU.add))
                    st.step(dve.tensor_scalar(pad[:], tile_of[:], float(NT), slot[:, CH:CH + 1], ALU.is_ge, ALU.mult))
                    st.settle()
                    st.step(dve.scalar_tensor_tensor(token0[:], tile_of[:], float(P), count[:], ALU.mult, ALU.add))
                    st.settle()
                    need(dve, x_idx_ready, g)
                    dve.tensor_tensor(token[:], token0[:], pad[:], ALU.add).then_inc(token_ready, 1)

                def x_indices(g):
                    dve.wait_ge(token_ready, g + 1)
                    need(dve, x_rows_in, 16 * CH * g)
                    if not isinstance(g, int) or g > 0:
                        dve.wait_ge(y_idx_ready, g)
                    dve.tensor_copy(x_idx[:], token[:]).then_inc(x_idx_ready, 1)

                def y_indices(g):
                    dve.wait_ge(x_idx_ready, g + 1)
                    need(dve, y_added, 32 * GRP * g)
                    st.step(dve.tensor_copy(y_idx[:], x_idx[:, 0:GRP]))
                    for k in range(GRP):
                        last = dve.tensor_copy(yt_idx[:, k:k + 1], x_idx[TAIL * k:TAIL * (k + 1), GRP:CH])
                        if k < GRP - 1:
                            st.step(last)
                    last.then_inc(y_idx_ready, 1)

                def gate_weights(g):
                    dve.wait_ge(x_rows_in, 16 * CH * (g + 1))
                    need(dve, y_ready, GRP * g)
                    for k in range(GRP):
                        col = bass.ds(g * GRP + (C + k), 1)
                        st.step(dve.tensor_copy(wy[:, k:k + 1], x_rows[:, k, col]))
                        last = dve.tensor_copy(wyt[:, k:k + 1], x_rows[TAIL * k:TAIL * (k + 1), GRP, col])
                        if k < GRP - 1:
                            st.step(last)
                    last.then_inc(wy_ready, 1)

                def product(g, k, s):
                    x = g * GRP + k
                    dve.wait_ge(silu_ready, 2 * x + s + 1)
                    need(dve, down_ready, x - 1)
                    dve.tensor_tensor(hT[k % 2][:, s * HF:(s + 1) * HF, :],
                                      up1[s][:, 0:HF * CAP].rearrange("p (f n) -> p f n", f=HF),
                                      silu[s][:].rearrange("p (f n) -> p f n", f=HF), ALU.mult).then_inc(h_ready, 1)

                def weigh(g, k):
                    x = g * GRP + k
                    dve.wait_ge(back_ready, x + 1)
                    if k == 0:
                        dve.wait_ge(wy_ready, g + 1)
                    need(dve, y_added, 32 * (x - GRP + 1))
                    st.step(dve.tensor_scalar(y[:, k, :], back[:, 0:C], wy[:, k:k + 1], None, ALU.mult))
                    dve.tensor_scalar(yt[:, k, :], back[0:TAIL, C:2 * C], wyt[:, k:k + 1], None, ALU.mult)\
                       .then_inc(y_ready, 1)

                dve.wait_ge(const_in, 16 * N_CONST)
                tiles_of(0)
                tokens_of(0)
                x_indices(0)
                y_indices(0)
                tiles_of(1)
                tokens_of(1)
                gate_weights(0)

                def turn(g, more):
                    if more >= 1:
                        x_indices(g + 1)
                    product(g, 0, 0)
                    if more >= 2:
                        tiles_of(g + 2)
                    product(g, 0, 1)
                    for k in range(1, GRP):
                        product(g, k, 0)
                        product(g, k, 1)
                        weigh(g, k - 1)
                        if k == 2 and more >= 2:
                            tokens_of(g + 2)
                    weigh(g, GRP - 1)
                    if more >= 1:
                        y_indices(g + 1)
                        gate_weights(g + 1)

                groups_loop(dve, turn, st)


HC = NH // 4
STACK = 3 * L
SHIFT = STACK + 2

CHUNKS = (3, 0, 1, 2)
BACK = [("o", c) for c in range(HC)] + [("yT", c) for c in range(CC)] + [("proj", u) for u in range(2)]
BY_SCALAR = ("xT", "q", "k", "yT")
SLOTS = [[("o", 0), ("o", 1), ("xT", 0), ("xT", 1)],
         [("q", 0), ("q", 1), ("o", 2), ("o", 3)],
         [("k", 0), ("k", 1), ("latq", 3), ("latq_s", 3)],
         [("latk", 3), ("latk_s", 3), ("yT", 0), ("yT", 1)],
         [("qk", 3), ("proj", 0), ("proj", 1)],
         [("latq", 0), ("latq_s", 0), ("latk", 0), ("latk_s", 0)],
         [("qk", 0), ("latq", 1), ("latq_s", 1), ("max", 12)],
         [("latk", 1), ("latk_s", 1), ("max", 13)],
         [("qk", 1), ("latq", 2), ("latq_s", 2), ("max", 14)],
         [("latk", 2), ("latk_s", 2), ("max", 15)],
         [("qk", 2), ("max", 0), ("max", 1)],
         [("max", 2), ("max", 3)],
         [("max", 4)],
         [("max", 5)],
         [("max", 6), ("max", 7)],
         [("max", 8), ("max", 9)],
         [("max", 10), ("max", 11)],
         [("v", 0), ("v", 1)]]


def read_before(items, n, scalar):
    return sum((name in BY_SCALAR) == scalar for name, _ in items[:n])


def attention(nc, tag, src, dst, a):
    scale = float(np.float32(L ** -0.5))
    FR = mybir.dt.float32r
    with ExitStack() as ctx:
        def sb(name, shape, dt=F32):
            return ctx.enter_context(nc.sbuf_tensor(f"{tag}_{name}", shape, dt))

        def sem(name):
            return nc.alloc_semaphore(f"{tag}_{name}")

        def bank(name):
            return ctx.enter_context(nc.psum_tensor(f"{tag}_{name}", [P, 512], F32))

        ident = sb("ident", [P, P])
        ident_b = sb("ident_b", [P, P], BF16)
        masks_f = sb("masks_f", [P, 2, P])
        masks = sb("masks", [P, 2, P], BF16)
        wqk_in = sb("wqk_in", [P, CC, 2 * C])
        latq_w = sb("latq_w", [P, 2, 2, P])
        latk_w = sb("latk_w", [P, 2, 2, P])
        qk_w = sb("qk_w", [P, P])
        cols = sb("cols", [P, 9])
        cos = sb("cos", [P, BLK])
        sin = sb("sin", [P, BLK])
        kv8 = sb("kv8", [L, P])
        l2o8 = sb("l2o8", [L, P])
        bmask = sb("bmask", [P, P])
        wv = sb("wv", [P, 2, C])
        bv = sb("bv", [P, 2])
        kvb = sb("kvb", [L, 1])
        l2ob = sb("l2ob", [P, C])
        at8 = sb("at8", [P, P])
        wvp = sb("wvp", [P, CC, C])
        bvb = sb("bvb", [P, 2, P])
        kvbb = sb("kvbb", [L, P])
        vbias = sb("vbias", [P, C])
        wp = sb("wp", [P, CC, C])
        pbias = sb("pbias", [P, C])
        xin = sb("xin", [P, TPB, C])
        xres = sb("xres", [P, TPB, C])
        xln = sb("xln", [P, TPB, C])
        xT = sb("xT", [P, CC, BLK])
        qT = sb("qT", [P, CC, BLK])
        kT = sb("kT", [P, CC, BLK])
        rot1 = sb("rot1", [P, BLK])
        rot2 = sb("rot2", [P, BLK])
        rotq = sb("rotq", [P, BLK])
        rotk = sb("rotk", [P, BLK])
        K_HI, K_LO, Q_HI, Q_LO = range(4)
        parts = [sb(f"parts{b}", [P, 4, BLK], FR) for b in range(2)]
        stacks = sb("stacks", [SHIFT, NH - 4, 2, BLK], FR)
        stacks3 = [sb(f"stacks3_{b}", [SHIFT, 4, 2, BLK], FR) for b in range(2)]
        v = sb("v", [P, TPB, NH, L])
        negmax = sb("negmax", [P, TPB, NH])
        m_hi = sb("m_hi", [NH, BLK], FR)
        m_lo = sb("m_lo", [NH, BLK], FR)
        PW = BLK + (BLK - P) + (BLK - 2 * P) + P
        PO = [0, BLK, BLK + BLK - P, PW - P]
        prob = [sb(f"prob{b}", [P, PW]) for b in range(2)]
        o_sb = sb("o", [P, HC, BLK])
        orec = sb("orec", [P, TPB, 4])
        ytok = sb("ytok", [P, TPB, C])
        yT = sb("yT", [P, CC, BLK])
        xout = sb("xout", [P, TPB, C])
        stats = sb("stats", [P, TPB, 6])
        mv = sb("mv", [P, TPB, 2])
        varp = sb("varp", [P, TPB])
        std = sb("std", [P, TPB])
        rstd = sb("rstd", [P, TPB])
        newton = sb("newton", [P, TPB])
        unused = sb("unused", [P, 1])

        work = [bank(f"work{b}") for b in range(2)]
        smax = [bank(f"smax{b}") for b in range(2)]
        score = [bank(f"score{b}") for b in range(3)]
        obank = bank("obank")

        const_in = sem("const_in")
        set_up = sem("set_up")
        set_mm = sem("set_mm")
        x_in = sem("x_in")
        xres_in = sem("xres_in")
        stack_in = [sem(f"stack_in{c}") for c in range(HC)]
        shift_in = sem("shift_in")
        out_kept = sem("out_kept")
        vec = sem("vec")
        var_ready = sem("var_ready")
        std_ready = sem("std_ready")
        ln_ready = sem("ln_ready")
        front_ready = sem("front_ready")
        front_act = sem("front_act")
        front_dve = sem("front_dve")
        back_ready = sem("back_ready")
        back_act = sem("back_act")
        back_dve = sem("back_dve")
        split_ready = sem("split_ready")
        rotq_ready = sem("rotq_ready")
        smax_ready = sem("smax_ready")
        smax_read = sem("smax_read")
        neg_ready = sem("neg_ready")
        m_ready = sem("m_ready")
        score_ready = sem("score_ready")
        exp_ready = sem("exp_ready")
        pv_ready = sem("pv_ready")
        o_out = sem("o_out")
        xres_ready = sem("xres_ready")
        N_CONST = 17
        items = [x for slot in SLOTS for x in slot if x[0] != "max"]
        front = [x for x in items if x not in BACK]
        assert len(items) % 2 == 0 and [x for x in items if x in BACK] == BACK
        assert items[-2:] == front[-2:] and not any(name in BY_SCALAR for name, _ in items[-2:])
        NFA, NFD = read_before(front, len(front), True), read_before(front, len(front), False)
        NBA, NBD = read_before(BACK, len(BACK), True), read_before(BACK, len(BACK), False)

        def slot_items(k, with_front, with_back):
            return [x for x in SLOTS[k] if x[0] != "max" and (with_back if x in BACK else with_front)]

        def slot_heads(k):
            return [h for name, h in SLOTS[k] if name == "max"]

        def bank_of(item):
            return work[items.index(item) % 2]

        def wait_ready(eng, i, item):
            if item in BACK:
                eng.wait_ge(back_ready, len(BACK) * i + BACK.index(item) + 1)
            else:
                eng.wait_ge(front_ready, len(front) * i + front.index(item) + 1)

        def taken_by(item):
            scalar = item[0] in BY_SCALAR
            if item in BACK:
                return (back_act, NBA, read_before(BACK, BACK.index(item) + 1, True)) if scalar else \
                       (back_dve, NBD, read_before(BACK, BACK.index(item) + 1, False))
            return (front_act, NFA, read_before(front, front.index(item) + 1, True)) if scalar else \
                   (front_dve, NFD, read_before(front, front.index(item) + 1, False))

        def wait_taken(eng, i, item):
            s, per, place = taken_by(item)
            eng.wait_ge(s, per * i + place)

        max_order = [h for slot in SLOTS for name, h in slot if name == "max"]
        MAX_AT = {h: n for n, h in enumerate(max_order)}

        def stacked(b, h):
            return stacks[:, h, :, :] if h < NH - 4 else stacks3[b.odd][:, h - (NH - 4), :, :]

        def turns_of(c):
            at = CHUNKS.index(c)
            return at % 2, CHUNKS[at - 2]

        with nc.Block() as block:

            @block.sync
            def _(sp):
                n = 0
                for dst_, s in ((ident, a["ident"]), (masks_f, a["masks"]), (wqk_in, a["wqkin"]),
                                (latq_w, a["latq"]), (latk_w, a["latk"]), (qk_w, a["qkw"]), (cols, a["cols"]),
                                (cos, a["cos"]), (sin, a["sin"]), (kv8, a["kv8"]), (l2o8, a["l2o8"]),
                                (bmask, a["bmask"]), (wv, a["wv"]), (bv, a["bv"]), (kvb, a["kvb"]),
                                (wp, a["wp"])):
                    sp.dma_start(dst_[:], s).then_inc(const_in, 16)
                    n += 1
                sp.dma_start(l2ob[:], a["l2ob"].unsqueeze(0).to_broadcast([P, C])).then_inc(const_in, 16)
                sp.dma_start(pbias[:], a["pbias"].unsqueeze(0).to_broadcast([P, C])).then_inc(const_in, 16)
                assert n + 2 == N_CONST + 1

                def load_x(i):
                    need(sp, ln_ready, i)
                    sp.dma_start(xin[:], token_major(src, i)).then_inc(x_in, 16)

                def stack(b, c):
                    own, _ = turns_of(c)
                    sp.wait_ge(split_ready, HC * b.i + CHUNKS.index(c) + 1)
                    need(sp, score_ready, 3 * (NH * (b.i - (2 if c == 3 else 1)) + 4 * c + 4))
                    for h in range(4):
                        rows = slice(L * h, L * (h + 1))
                        for r, (k_part, q_part) in enumerate(((K_HI, Q_HI), (K_LO, Q_HI), (K_HI, Q_LO))):
                            sp.dma_start(stacked(b, 4 * c + h)[L * r:L * (r + 1), :, :].bitcast(F32),
                                         parts[own][rows, k_part:q_part + 1:q_part - k_part, :].bitcast(F32))\
                                .then_inc(stack_in[c], 16)

                def shift(b):
                    sp.wait_ge(m_ready, b.i + 1)
                    for r, part in ((STACK, m_hi), (STACK + 1, m_lo)):
                        sp.dma_start(stacks[r:r + 1, :, 1, :].bitcast(F32), part[0:NH - 4, :].bitcast(F32))\
                            .then_inc(shift_in, 16)
                        sp.dma_start(stacks3[b.odd][r:r + 1, :, 1, :].bitcast(F32), part[NH - 4:NH, :].bitcast(F32))\
                            .then_inc(shift_in, 16)

                def keep_out(i):
                    sp.wait_ge(back_dve, NBD * (i + 1))
                    sp.dma_start(token_major(dst, i), xout[:]).then_inc(out_kept, 16)

                load_x(0)
                load_x(1)
                for c in CHUNKS:
                    stack(Blk(0, 0), c)
                shift(Blk(0, 0))

                def turn(b, more):
                    i = b.i
                    if more >= 2:
                        load_x(i + 2)
                    if more:
                        stack(b.plus(1), CHUNKS[0])
                    if not isinstance(i, int) or i > 0:
                        keep_out(i - 1)
                    sp.dma_start(xres[:], token_major(src, i)).then_inc(xres_in, 16)
                    if more:
                        for c in CHUNKS[1:]:
                            stack(b.plus(1), c)
                        shift(b.plus(1))

                pairs_loop(nc, sp, BATCH, turn)
                keep_out(BATCH - 1)
                sp.wait_ge(out_kept, 16 * BATCH)

            @block.tensor
            def _(pe):
                def to_bank(i, item, with_front, with_back):
                    turn_i = i + 1 if item in BACK else i - 1
                    at = items.index(item)
                    before = [x for x in items[at % 2:at:2] if (with_back if x in BACK else with_front)]
                    if before:
                        x = before[-1]
                        wait_taken(pe, turn_i + (-1 if x in BACK else 1), x)
                    else:
                        need(pe, front_dve, NFD * (turn_i + 1))
                    return bank_of(item)

                def front_item(i, item, with_back):
                    name, c = item
                    if name == "xT" and c == 0:
                        pe.wait_ge(ln_ready, i + 1)
                    if (name, c) == ("q", 0):
                        wait_taken(pe, i, ("xT", CC - 1))
                    if (name, c) == ("latq", CHUNKS[0]):
                        wait_taken(pe, i, ("q", CC - 1))
                    if (name, c) == ("latk", CHUNKS[0]):
                        wait_taken(pe, i, ("k", CC - 1))
                    if name == "qk":
                        pe.wait_ge(rotq_ready, HC * i + CHUNKS.index(c) + 1)
                    w = to_bank(i, item, True, with_back)
                    if name == "xT":
                        for t in range(TPB):
                            last = pe.transpose(w[:, t * P:(t + 1) * P], xln[:, t, c * P:(c + 1) * P], ident[:])
                    elif name in ("q", "k"):
                        o = (C if name == "k" else 0) + c * P
                        for h in range(CC):
                            last = pe.matmul(w[:], wqk_in[:, h, o:o + P], xT[:, h, :],
                                             start=(h == 0), stop=(h == CC - 1))
                    elif name == "v":
                        for t in range(2):
                            tok = (2 * c + t) * P
                            for h in range(CC):
                                last = pe.matmul(w[:, t * C:(t + 1) * C], xT[:, h, tok:tok + P], wvp[:, h, :],
                                                 start=(h == 0), stop=(h == CC - 1))
                    elif name == "qk":
                        last = pe.matmul(w[:], qk_w[:], rotq[:], start=True, stop=True)
                    else:
                        lw, x = (latq_w, qT) if "q" in name[3:4] else (latk_w, kT)
                        last = pe.matmul(w[:], lw[:, c % 2, int(name.endswith("_s")), :], x[:, c // 2, :],
                                         start=True, stop=True)
                    last.then_inc(front_ready, 1)

                def max_tile(b, h, t):
                    if h % 4 == 0 and t == 0:
                        pe.wait_ge(stack_in[h // 4], 16 * 12 * (b.i + 1))
                    if h == 4 * CHUNKS[0] and t == 0:
                        need(pe, m_ready, b.i)
                    n = TPB * (NH * b.i + MAX_AT[h]) + t
                    need(pe, smax_read, n - 1)
                    s, st_ = smax[t % 2], stacked(b, h)
                    pe.matmul(s[:, 0:(t + 1) * P], st_[0:STACK, 1, t * P:(t + 1) * P],
                              st_[0:STACK, 0, 0:(t + 1) * P], start=True, stop=False)
                    pe.matmul(s[:, t * P:(t + 1) * P], ident_b[:], masks[:, 0, :], start=False, stop=True)\
                      .then_inc(smax_ready, 1)

                def turn_maxima(i):
                    pe.wait_ge(smax_read, TPB * NH * (i + 1))
                    for t in range(TPB):
                        last = pe.transpose(smax[0][0:NH, t * P:(t + 1) * P], negmax[:, t, :], ident[:])
                    last.then_inc(neg_ready, 1)

                def scores(b, h):
                    x = NH * b.i + h
                    if h == 0:
                        pe.wait_ge(shift_in, 64 * (b.i + 1))
                    st_ = stacked(b, h)
                    for kt in range(TPB):
                        s, o = (score[kt], 0) if kt < 3 else (score[2], BLK - 2 * P)
                        if kt < 3:
                            need(pe, exp_ready, 3 * (x - 1) + kt + 1)
                        pe.matmul(s[:, o:o + BLK - kt * P], st_[:, 0, kt * P:(kt + 1) * P], st_[:, 1, kt * P:BLK],
                                  start=True, stop=False)
                        last = pe.matmul(s[:, o:o + P], ident_b[:], masks[:, 1, :], start=False, stop=True)
                        if kt != 2:
                            last.then_inc(score_ready, 1)

                def weighted(i, h, kt):
                    x = NH * i + h
                    if kt < 3:
                        pe.wait_ge(exp_ready, 3 * x + kt + 1)
                    if kt == 0:
                        if h == 0:
                            wait_taken(pe, i, ("v", 1))
                            need(pe, o_out, HC * i)
                        elif h % 4 == 0:
                            pe.wait_ge(o_out, HC * i + h // 4)
                    q = L * (h % 4)
                    last = pe.matmul(obank[q:q + L, kt * P:BLK], v[:, kt, h, :],
                                     prob[h % 2][:, PO[kt]:PO[kt] + BLK - kt * P],
                                     start=(kt == 0), stop=(kt == TPB - 1))
                    if kt == TPB - 1:
                        last.then_inc(pv_ready, 1)

                def back_item(i, item, w):
                    name, c = item
                    if name == "o":
                        pe.wait_ge(o_out, HC * i + c + 1)
                        for t in range(TPB):
                            last = pe.transpose(w[:, t * P:(t + 1) * P], o_sb[:, c, t * P:(t + 1) * P], ident[:])
                    elif name == "yT":
                        if c == 0:
                            wait_taken(pe, i, ("o", HC - 1))
                        for t in range(TPB):
                            last = pe.transpose(w[:, t * P:(t + 1) * P], ytok[:, t, c * P:(c + 1) * P], ident[:])
                    else:
                        if c == 0:
                            wait_taken(pe, i, ("yT", CC - 1))
                        for t in range(2):
                            tok = (2 * c + t) * P
                            for h in range(CC):
                                last = pe.matmul(w[:, t * C:(t + 1) * C], yT[:, h, tok:tok + P], wp[:, h, :],
                                                 start=(h == 0), stop=(h == CC - 1))
                    last.then_inc(back_ready, 1)

                pe.wait_ge(const_in, 16 * (N_CONST + 1))
                pe.matmul(work[0][:, 0:P], kv8[:], l2o8[:], start=True, stop=True).then_inc(set_mm, 1)
                pe.wait_ge(set_up, 1)
                for h in range(CC):
                    for g in range(2):
                        pe.matmul(work[1][:, h * C + g * P:h * C + (g + 1) * P], wv[:, g, h * P:(h + 1) * P],
                                  at8[:], start=True, stop=True)
                for g in range(2):
                    pe.matmul(score[0][:, g * P:(g + 1) * P], bvb[:, g, :], at8[:], start=True, stop=False)
                    last = pe.matmul(score[0][:, g * P:(g + 1) * P], kvbb[:], l2o8[:], start=False, stop=True)
                last.then_inc(set_mm, 1)
                pe.wait_ge(set_up, 2)

                for k in range(len(SLOTS)):
                    for item in slot_items(k, True, False):
                        front_item(0, item, False)
                    for h in slot_heads(k):
                        for t in range(TPB):
                            max_tile(Blk(0, 0), h, t)
                turn_maxima(0)

                def turn(b, more):
                    i = b.i
                    with_front, with_back = more > 0, not isinstance(i, int) or i > 0

                    def banked(k):
                        for item in slot_items(k, with_front, with_back):
                            if item in BACK:
                                back_item(i - 1, item, to_bank(i - 1, item, with_front, with_back))
                            else:
                                front_item(i + 1, item, with_back)

                    banked(0)
                    for h in range(NH):
                        scores(b, h)
                        banked(h + 1)
                        tiles = [(m, t) for m in slot_heads(h + 1) for t in range(TPB)] if more else []
                        per = len(tiles) // TPB
                        for kt in range(TPB):
                            for m, t in tiles[kt * per:(kt + 1) * per]:
                                max_tile(b.plus(1), m, t)
                            if h:
                                weighted(i, h - 1, kt)
                    if more:
                        turn_maxima(i + 1)
                    for kt in range(TPB):
                        weighted(i, NH - 1, kt)
                    banked(NH + 1)

                pairs_loop(nc, pe, BATCH, turn)
                wait_taken(pe, BATCH - 2, BACK[-1])
                for n, item in enumerate(BACK):
                    if n >= 2:
                        wait_taken(pe, BATCH - 1, BACK[n - 2])
                    back_item(BATCH - 1, item, bank_of(item))

            @block.scalar
            def _(act):
                def std_of(i):
                    act.wait_ge(var_ready, i + 1)
                    act.activation(std[:], varp[:], ACT.Sqrt).then_inc(std_ready, 1)

                def take(i, item):
                    name, c = item
                    if name not in BY_SCALAR:
                        return
                    wait_ready(act, i, item)
                    w = bank_of(item)
                    if name == "xT":
                        act.activation(xT[:, c, :], w[:], ACT.Copy).then_inc(front_act, 1)
                    elif name == "q":
                        act.activation(qT[:, c, :], w[:], ACT.Identity, bias=cols[:, c:c + 1]).then_inc(front_act, 1)
                    elif name == "k":
                        act.activation(kT[:, c, :], w[:], ACT.Identity, bias=cols[:, 2 + c:3 + c])\
                           .then_inc(front_act, 1)
                    else:
                        act.activation(yT[:, c, :], w[:], ACT.Copy).then_inc(back_act, 1)

                def exps(i, h):
                    x = NH * i + h
                    need(act, pv_ready, x - 1)
                    for j, width in ((0, BLK), (1, BLK - P), (2, BLK - P)):
                        act.wait_ge(score_ready, 3 * x + j + 1)
                        act.activation(prob[h % 2][:, PO[j]:PO[j] + width], score[j][:, 0:width], ACT.Exp,
                                       scale=scale).then_inc(exp_ready, 1)

                def o_take(i, c):
                    act.wait_ge(pv_ready, NH * i + 4 * c + 4)
                    if c == 0:
                        need(act, back_ready, len(BACK) * (i - 1) + HC)
                    act.activation(o_sb[:, c, :], obank[:], ACT.Copy).then_inc(o_out, 1)

                act.wait_ge(const_in, 16 * (N_CONST + 1))
                std_of(0)
                std_of(1)
                for item in front:
                    take(0, item)

                def turn(b, more):
                    i = b.i

                    def banked(k):
                        for item in slot_items(k, more > 0, not isinstance(i, int) or i > 0):
                            take(i - 1 if item in BACK else i + 1, item)

                    banked(0)
                    for h in range(NH):
                        exps(i, h)
                        banked(h + 1)
                        if h % 4 == 1 and h > 4:
                            o_take(i, h // 4 - 1)
                        if h == 11 and more >= 2:
                            std_of(i + 2)
                    o_take(i, HC - 1)
                    banked(NH + 1)

                pairs_loop(nc, act, BATCH, turn)
                for item in BACK:
                    take(BATCH - 1, item)

            @block.gpsimd
            def _(pool):
                def turn(b, more):
                    pool.wait_ge(xres_in, 16 * (b.i + 1))
                    pool.tensor_tensor(xres[:], xres[:], pbias[:].unsqueeze(1).to_broadcast([P, TPB, C]), ALU.add)\
                        .then_inc(xres_ready, 1)

                pool.wait_ge(const_in, 16 * (N_CONST + 1))
                pairs_loop(nc, pool, BATCH, turn)

            @block.vector
            def _(dve):
                st = Steps(dve, vec)

                def ln_stats(i):
                    dve.wait_ge(x_in, 16 * (i + 1))
                    for t in range(TPB):
                        st.step(dve.bn_stats(stats[:, t, :], xin[:, t, :]))
                    st.settle_on(unused[:])
                    for t in range(TPB):
                        st.step(dve.bn_aggr(mv[:, t, :], stats[:, t, :]))
                    st.settle()
                    need(dve, std_ready, i)
                    dve.tensor_scalar(varp[:], mv[:, :, 1], EPS, None, ALU.add).then_inc(var_ready, 1)

                def ln_apply(i):
                    dve.wait_ge(std_ready, i + 1)
                    rsqrt_refined(dve, st, rstd, varp, std, newton)
                    need(dve, front_act, (i - 1) * NFA + 2)
                    for t in range(TPB):
                        last = dve.tensor_scalar(xln[:, t, :], xin[:, t, :], mv[:, t, 0:1],
                                                 rstd[:, t:t + 1], ALU.subtract, ALU.mult)
                        if t < TPB - 1:
                            st.step(last)
                    last.then_inc(ln_ready, 1)

                def take(i, item):
                    name, c = item
                    if name in BY_SCALAR:
                        return
                    wait_ready(dve, i, item)
                    w = bank_of(item)
                    if name == "v":
                        if c == 0:
                            need(dve, pv_ready, NH * i)
                        for t in range(2):
                            last = dve.tensor_tensor(v[:, 2 * c + t, :, 0:HD],
                                                     w[:, t * C:(t + 1) * C].rearrange("p (h d) -> p h d", h=NH),
                                                     vbias[:].rearrange("p (h d) -> p h d", h=NH), ALU.add)
                            if t == 0:
                                st.step(last)
                        last.then_inc(front_dve, 1)
                    elif name == "o":
                        heads = w[:].rearrange("p (t h l) -> p t h l", t=TPB, h=4)
                        need(dve, back_dve, NBD * i + c)
                        st.step(dve.reciprocal(orec[:], heads[:, :, :, HD]))
                        st.settle()
                        dve.tensor_tensor(ytok[:, :, c * 64:(c + 1) * 64].rearrange("p t (h d) -> p t h d", h=4),
                                          heads[:, :, :, 0:HD], orec[:].unsqueeze(3).to_broadcast([P, TPB, 4, HD]),
                                          ALU.mult).then_inc(back_dve, 1)
                    elif name == "proj":
                        if c == 0:
                            dve.wait_ge(xres_ready, i + 1)
                            need(dve, out_kept, 16 * i)
                        dve.tensor_tensor(xout[:, 2 * c:2 * c + 2, :], w[:].rearrange("p (t n) -> p t n", t=2),
                                          xres[:, 2 * c:2 * c + 2, :], ALU.add).then_inc(back_dve, 1)
                    elif name == "qk":
                        bias = cols[:, 8:9]
                        own, before = turns_of(c)
                        p_ = parts[own]
                        need(dve, stack_in[before], 16 * 12 * (i + (CHUNKS.index(c) >= 2)))
                        st.step(dve.tensor_scalar(p_[:, Q_HI, :], w[:], bias, None, ALU.add))
                        st.step(dve.tensor_copy(p_[:, K_HI, :], rotk[:]))
                        st.settle()
                        dve.scalar_tensor_tensor(p_[:, Q_LO, :], w[:], bias, p_[:, Q_HI, :].bitcast(F32), ALU.add,
                                                 ALU.subtract).then_inc(front_dve, 1)
                        dve.tensor_tensor(p_[:, K_LO, :], rotk[:], p_[:, K_HI, :].bitcast(F32), ALU.subtract)\
                           .then_inc(split_ready, 1)
                    else:
                        is_q, swapped = name[3] == "q", name.endswith("_s")
                        bias = cols[:, (4 if is_q else 6) + swapped:(5 if is_q else 7) + swapped]
                        if not swapped:
                            dve.scalar_tensor_tensor(rot1[:], w[:], bias, cos[:], ALU.add, ALU.mult)\
                               .then_inc(front_dve, 1)
                        else:
                            dve.scalar_tensor_tensor(rot2[:], w[:], bias, sin[:], ALU.add, ALU.mult)\
                               .then_inc(front_dve, 1)
                            wait_taken(dve, i, item)
                            if is_q:
                                dve.tensor_tensor(rotq[:], rot1[:], rot2[:], ALU.add).then_inc(rotq_ready, 1)
                                dve.wait_ge(rotq_ready, HC * i + CHUNKS.index(c) + 1)
                            else:
                                need(dve, split_ready, HC * i + CHUNKS.index(c))
                                st.step(dve.tensor_tensor(rotk[:], rot1[:], rot2[:], ALU.add))
                            st.settle()

                def maxima(i, h):
                    for t in range(TPB):
                        n = TPB * (NH * i + MAX_AT[h]) + t
                        dve.wait_ge(smax_ready, n + 1)
                        if MAX_AT[h] == 0 and t == 0:
                            need(dve, neg_ready, i)
                        dve.tensor_reduce(negmax[:, t, h:h + 1], smax[t % 2][:, 0:(t + 1) * P], AX.X, ALU.max,
                                          negate=True).then_inc(smax_read, 1)

                def split_maxima(i):
                    dve.wait_ge(neg_ready, i + 1)
                    need(dve, shift_in, 64 * i)
                    st.step(dve.tensor_copy(m_hi[:], smax[0][0:NH, :]))
                    st.settle()
                    dve.tensor_tensor(m_lo[:], smax[0][0:NH, :], m_hi[:].bitcast(F32), ALU.subtract)\
                       .then_inc(m_ready, 1)

                dve.wait_ge(const_in, 16 * (N_CONST + 1))
                st.step(dve.tensor_copy(ident_b[:], ident[:]))
                st.step(dve.tensor_copy(masks[:], masks_f[:]))
                st.step(dve.memset(v[:], 0.0))
                for x in [stacks] + stacks3:
                    st.step(dve.memset(x[STACK:SHIFT, :, 0, :].bitcast(F32), 1.0))
                st.settle()
                st.step(dve.memset(v[:, :, :, HD:HD + 1], 1.0))
                st.step(dve.memset(bvb[:], 0.0))
                st.step(dve.memset(kvbb[:], 0.0))
                st.settle()
                for g in range(2):
                    st.step(dve.tensor_scalar(bvb[:, g, :], bvb[:, g, :], bv[:, g:g + 1], None, ALU.add))
                st.step(dve.tensor_scalar(kvbb[:], kvbb[:], kvb[:], None, ALU.add))
                dve.wait_ge(set_mm, 1)
                st.settle()
                dve.tensor_tensor(at8[:], work[0][:, 0:P], bmask[:], ALU.mult).then_inc(set_up, 1)
                dve.wait_ge(set_mm, 2)
                st.step(dve.tensor_copy(wvp[:], work[1][:].rearrange("p (c n) -> p c n", c=CC)))
                dve.tensor_tensor(vbias[:], score[0][:, 0:C], l2ob[:], ALU.add).then_inc(set_up, 1)
                dve.wait_ge(set_up, 2)
                ln_stats(0)
                ln_apply(0)
                ln_stats(1)
                for k in range(len(SLOTS)):
                    for item in slot_items(k, True, False):
                        take(0, item)
                    for h in slot_heads(k):
                        maxima(0, h)
                ln_apply(1)
                split_maxima(0)

                def turn(b, more):
                    i = b.i
                    for k in range(len(SLOTS)):
                        if k == len(SLOTS) - 1 and more:
                            split_maxima(i + 1)
                        for item in slot_items(k, more > 0, not isinstance(i, int) or i > 0):
                            take(i - 1 if item in BACK else i + 1, item)
                        if more:
                            for h in slot_heads(k):
                                maxima(i + 1, h)
                        if k == 11 and more >= 2:
                            ln_stats(i + 2)
                        if k == 13 and more >= 2:
                            ln_apply(i + 2)

                pairs_loop(nc, dve, BATCH, turn, st)
                for item in BACK:
                    take(BATCH - 1, item)


def program(nc, a):
    def scratch(name, shape):
        return nc.dram_tensor(name, shape, F32, kind="Internal").ap()

    xtab = scratch("xtab", [TOK + P, ROW])
    cumtab = scratch("cumtab", [(NT + 1) * E, P])
    cend = scratch("cend", [E, NT])
    x1 = scratch("x1", [TOK + P, C])
    x2 = scratch("x2", [TOK, C])
    ffn_dense(nc, "d1", a["x"], x1, xtab, cumtab, cend, a)
    ffn_routed(nc, "r1", x1, xtab, cumtab, cend, a)
    attention(nc, "at", x1, x2, a)
    ffn_dense(nc, "d2", x2, a["out"], xtab, cumtab, cend, a)
    ffn_routed(nc, "r2", a["out"], xtab, cumtab, cend, a)


def laid_out(v):
    f = {k: np.asarray(x) for k, x in v.items()}

    def image(w):
        return np.ascontiguousarray(w.T.reshape(-1, P, w.shape[0]).transpose(1, 0, 2))

    part = np.arange(P)
    pair = np.arange(L) ^ 1
    m = {"x": np.ascontiguousarray(f["L0_attn_x"].reshape(TOK, C)), "wg": image(f["L0_ffn_wg"]),
         "sw1": image(f["L0_ffn_shared_w1"]), "sw2": image(f["L0_ffn_shared_w2"])}
    w1, w2 = f["L0_ffn_expert_w1"], f["L0_ffn_expert_w2"]
    m["experts"] = np.concatenate(
        [w1.transpose(0, 2, 1).reshape(E, CC, P, 2 * F).transpose(0, 2, 1, 3).reshape(E, P, CC * 2 * F),
         w2.transpose(0, 2, 1).reshape(E, FC, P, C).transpose(0, 2, 1, 3).reshape(E, P, FC * C)], 2)
    m["ident"] = np.eye(P, dtype=np.float32)
    tri = np.zeros((P, TPB, BLK), np.float32)
    for t in range(TPB):
        tri[:, t, :] = np.arange(BLK)[None, :] >= t * P + part[:, None]
    m["tri"] = tri
    m["slot"] = np.stack([part] * GRP + [P + part % TAIL, part], 1).astype(np.float32)
    first = GRP * np.arange(NG)
    m["erow"] = np.stack([np.broadcast_to(first + k, (P, NG)) for k in range(GRP)]
                         + [first[None] + part[:, None] // TAIL], 2).astype(np.float32)
    wa, ba = f["L0_attn_c_attn_w"], f["L0_attn_c_attn_b"]
    m["wqkin"] = image(wa[0:2 * C])
    for name, w in (("latq", f["L0_attn_q2l_w"]), ("latk", f["L0_attn_kv2l_w"])):
        lat = np.zeros((P, 2, 2, P), np.float32)
        for half in range(2):
            for h in range(4):
                rows = slice(64 * half + HD * h, 64 * half + HD * (h + 1))
                lat[rows, half, 0, L * h:L * (h + 1)] = w.T
                lat[rows, half, 1, L * h:L * (h + 1)] = w[pair].T
        m[name] = lat
    qkw = np.zeros((P, P), np.float32)
    for h in range(4):
        qkw[L * h:L * (h + 1), L * h:L * (h + 1)] = f["L0_attn_wqk_w"].T
    m["qkw"] = qkw
    qb, kb = f["L0_attn_q2l_b"], f["L0_attn_kv2l_b"]
    m["cols"] = np.stack([ba[0:P], ba[P:C], ba[C:C + P], ba[C + P:2 * C], np.tile(qb, 4), np.tile(qb[pair], 4),
                          np.tile(kb, 4), np.tile(kb[pair], 4), np.tile(f["L0_attn_wqk_b"], 4)], 1)
    inv = (1.0 / 10000.0 ** (np.arange(0, L, 2, dtype=np.float32) / np.float32(L))).astype(np.float32)
    freqs = np.outer(np.arange(SEQ, dtype=np.float32), inv).astype(np.float32)
    sign = np.where(np.arange(L) % 2 == 0, -1.0, 1.0).astype(np.float32)
    m["cos"] = np.tile(np.repeat(np.cos(freqs), 2, axis=1).T, (4, 1)).astype(np.float32)
    m["sin"] = np.tile(np.repeat(np.sin(freqs), 2, axis=1).T * sign[:, None], (4, 1)).astype(np.float32)
    m["kv8"] = np.tile(f["L0_attn_kv2l_w"], (1, 8))
    m["l2o8"] = np.tile(f["L0_attn_l2o_w"].T, (1, 8))
    m["bmask"] = (part[:, None] // HD == part[None] // HD).astype(np.float32)
    m["wv"] = np.ascontiguousarray(wa[2 * C:].reshape(2, P, C).transpose(1, 0, 2))
    m["bv"] = np.ascontiguousarray(ba[2 * C:].reshape(2, P).T)
    m["kvb"] = np.ascontiguousarray(kb[:, None])
    m["l2ob"] = np.tile(f["L0_attn_l2o_b"], NH)
    m["wp"] = image(f["L0_attn_cproj_w"])
    m["pbias"] = f["L0_attn_cproj_b"]
    hidden = np.where(part[None] > part[:, None], -1.0e30, 0.0)
    m["masks"] = np.stack([hidden, hidden.T], 1).astype(np.float32)
    return {k: np.ascontiguousarray(x) for k, x in m.items()}


def kernel(**inputs):
    import concourse.bacc as bacc
    from concourse.bass_utils import run_bass_kernel_spmd

    arrays = laid_out(inputs)
    nc = bacc.Bacc("TRN2", target_bir_lowering=False, num_devices=1)
    args = {k: nc.dram_tensor(f"in_{k}", x.shape, F32, kind="ExternalInput").ap() for k, x in arrays.items()}
    args["out"] = nc.dram_tensor("out_0", (TOK + P, C), F32, kind="ExternalOutput").ap()
    program(nc, args)
    r = run_bass_kernel_spmd(nc, [{f"in_{k}": x for k, x in arrays.items()}], core_ids=[0])
    return r.results[0]["out_0"][0:TOK].reshape(BATCH, SEQ, C)
```

```python
from contextlib import ExitStack

import numpy as np

import concourse.bass as bass
from concourse import mybir

ALU = mybir.AluOpType
ACT = mybir.ActivationFunctionType
AX = mybir.AxisListType
F32 = mybir.dt.float32
BF16 = mybir.dt.bfloat16
I32 = mybir.dt.int32

P = 128
BATCH, SEQ, C = 16, 512, 256
TOK = BATCH * SEQ
CC = C // P
E, TOPK, CAP, F = 64, 8, 160, 768
FC = F // P
BLK = 512
TPB = BLK // P
NBLK = TOK // BLK
NT = TOK // P
ROW = C + E
GRP = 4
NG = E // GRP
TAIL = CAP - P
NH, HD, L = 16, 16, 32
EPS = 1e-5
FLT_EPS = float(np.finfo(np.float32).eps)


def need(eng, sem, value):
    if isinstance(value, int) and value <= 0:
        return
    eng.wait_ge(sem, value)


class Steps:

    def __init__(self, eng, sem):
        self.eng, self.sem, self.base, self.n = eng, sem, 0, 0

    def step(self, instruction):
        instruction.then_inc(self.sem, 1)
        self.n += 1

    def settle(self):
        need(self.eng, self.sem, self.base + self.n)

    def settle_on(self, cell):
        self.settle()
        self.eng.memset(cell, 0.0)

    def loop(self, turn, per_turn):
        self.base, self.entry, self.n = self.base + self.n + turn * per_turn, self.n + self.base, 0
        self.per_turn = per_turn

    def end_loop(self, turns):
        assert self.n == self.per_turn, (self.n, self.per_turn)
        self.base, self.n = self.entry + turns * self.per_turn, 0


def rsqrt_refined(dve, st, out, var, std, tmp):
    for step in (lambda: dve.reciprocal(out[:], std[:]),
                 lambda: dve.tensor_tensor(tmp[:], out[:], out[:], ALU.mult),
                 lambda: dve.tensor_tensor(tmp[:], tmp[:], var[:], ALU.mult),
                 lambda: dve.tensor_scalar(tmp[:], tmp[:], -0.5, 1.5, ALU.mult, ALU.add),
                 lambda: dve.tensor_tensor(out[:], out[:], tmp[:], ALU.mult)):
        st.step(step())
        st.settle()


class Blk:

    def __init__(self, pair, odd):
        self.pair, self.odd = pair + odd // 2, odd % 2
        self.i = self.pair * 2 + self.odd

    def plus(self, k):
        return Blk(self.pair, self.odd + k)


def pairs_loop(nc, eng, n_blocks, body, steps=None):
    body(Blk(0, 0), 2)
    start = steps.n if steps else 0
    body(Blk(0, 1), 2)
    per = 2 * (steps.n - start) if steps else 0
    turns = n_blocks // 2 - 2
    with eng.Fori(1, 1 + turns) as pair:
        if steps:
            steps.loop(pair - 1, per)
        body(Blk(pair, 0), 2)
        body(Blk(pair, 1), 2)
    if steps:
        steps.end_loop(turns)
    body(Blk(n_blocks // 2 - 1, 0), 1)
    body(Blk(n_blocks // 2 - 1, 1), 0)


def token_major(dram, i):
    return dram[bass.ds(i * BLK, BLK), :].rearrange("(t p) n -> p t n", p=P)


def ffn_dense(nc, tag, src, acc, xtab, cumtab, cend_dram, a):
    FR = mybir.dt.float32r
    with ExitStack() as ctx:
        def sb(name, shape, dt=F32):
            return ctx.enter_context(nc.sbuf_tensor(f"{tag}_{name}", shape, dt))

        def sem(name):
            return nc.alloc_semaphore(f"{tag}_{name}")

        ident = sb("ident", [P, P])
        tri_f = sb("tri_f", [P, TPB, BLK])
        tri = sb("tri", [P, TPB, BLK], BF16)
        wg_sb = sb("wg", [P, CC, E])
        w1_hi = sb("w1_hi", [P, CC, 2 * F], FR)
        w1_lo = sb("w1_lo", [P, CC, 2 * F], FR)
        w2 = sb("w2", [P, FC, C])
        xin = [sb(f"xin{b}", [P, TPB, C]) for b in range(2)]
        xres = [sb(f"xres{b}", [P, TPB, C]) for b in range(2)]
        xln = [sb(f"xln{b}", [P, TPB, C]) for b in range(2)]
        xT = [sb(f"xT{b}", [P, CC, BLK]) for b in range(2)]
        xT_hi = [sb(f"xT_hi{b}", [P, CC, BLK], FR) for b in range(2)]
        xT_lo = [sb(f"xT_lo{b}", [P, CC, BLK], FR) for b in range(2)]
        hT = [sb(f"hT{b}", [P, FC, BLK]) for b in range(2)]
        w1 = hT[0][:].rearrange("p f n -> p (f n)").rearrange("p (c f) -> p c f", c=CC)
        assert FC * BLK == CC * 2 * F
        silu = [sb(f"silu{b}", [P, BLK]) for b in range(2)]
        xout = [sb(f"xout{b}", [P, TPB, C]) for b in range(2)]
        gates_out = [sb(f"gates_out{b}", [P, TPB, E]) for b in range(2)]
        cum_sb = [sb(f"cum{b}", [E, BLK]) for b in range(2)]
        carry = sb("carry", [E, 1])
        cend = sb("cend", [E, NT])
        stats = sb("stats", [P, TPB, 6])
        mv = sb("mv", [P, TPB, 2])
        varp = sb("varp", [P, TPB])
        std = sb("std", [P, TPB])
        rstd = sb("rstd", [P, TPB])
        newton = sb("newton", [P, TPB])
        negmax = sb("negmax", [P, TPB])
        zlog = sb("zlog", [P, TPB, E])
        ez = sb("ez", [P, TPB, E])
        gate = sb("gate", [P, TPB, E])
        struck = sb("struck", [P, TPB, E])
        gscaled = sb("gscaled", [P, TPB, E])
        mask = sb("mask", [P, TPB, E], BF16)
        top8 = sb("top8", [P, TPB, TOPK])
        esum = sb("esum", [P, TPB])
        rsum = sb("rsum", [P, TPB])
        tsum = sb("tsum", [P, TPB])
        tclip = sb("tclip", [P, TPB])
        trec = sb("trec", [P, TPB])
        thalf = sb("thalf", [P, TPB])
        unused = sb("unused", [P, 1])
        zrow = sb("zrow", [P, ROW])
        brow = sb("brow", [E, P])

        def bank(name):
            return ctx.enter_context(nc.psum_tensor(f"{tag}_{name}", [P, 512], F32))

        side = [bank(f"side{c}") for c in range(2)]
        up1 = [bank(f"up1_{b}") for b in range(2)]
        up2 = [bank(f"up2_{b}") for b in range(2)]
        down = [bank(f"down{b}") for b in range(2)]

        const_in = sem("const_in")
        first_in = sem("first_in")
        w1_hi_ready = sem("w1_hi_ready")
        set_up = sem("set_up")
        x_in = [sem(f"x_in{b}") for b in range(2)]
        xres_in = [sem(f"xres_in{b}") for b in range(2)]
        tables_kept = [sem(f"tables_kept{b}") for b in range(2)]
        out_kept = [sem(f"out_kept{b}") for b in range(2)]
        pad_kept = sem("pad_kept")
        pads_set = sem("pads_set")
        vec = sem("vec")
        var_ready = sem("var_ready")
        std_ready = sem("std_ready")
        ln_ready = sem("ln_ready")
        turned = sem("turned")
        xT_ready = sem("xT_ready")
        xT_hi_ready = sem("xT_hi_ready")
        xT_split = sem("xT_split")
        logits_ready = sem("logits_ready")
        logits_read = sem("logits_read")
        ez_ready = sem("ez_ready")
        route_ready = sem("route_ready")
        cum_ready = sem("cum_ready")
        cum_read = sem("cum_read")
        up_ready = sem("up_ready")
        silu_ready = sem("silu_ready")
        h_ready = sem("h_ready")
        down_ready = sem("down_ready")
        out_ready = sem("out_ready")
        N_FIRST, N_CONST = 3, 2

        with nc.Block() as block:

            @block.sync
            def _(sp):
                def load_x(b):
                    need(sp, ln_ready, b.i - 1)
                    sp.dma_start(xin[b.odd][:], token_major(src, b.i)).then_inc(x_in[b.odd], 16)

                load_x(Blk(0, 0))
                sp.dma_start(ident[:], a["ident"]).then_inc(first_in, 16)
                sp.dma_start(wg_sb[:], a["wg"]).then_inc(first_in, 16)
                sp.dma_start(w1, a["sw1"]).then_inc(first_in, 16)
                load_x(Blk(0, 1))
                for dst, s in ((tri_f, a["tri"]), (w2, a["sw2"])):
                    sp.dma_start(dst[:], s).then_inc(const_in, 16)
                sp.wait_ge(pads_set, 2)
                sp.dma_start(xtab[TOK:TOK + P, :], zrow[:]).then_inc(pad_kept, 16)
                sp.dma_start(acc[TOK:TOK + P, :], zrow[:, 0:C]).then_inc(pad_kept, 16)
                sp.dma_start(cumtab[NT * E:(NT + 1) * E, :], brow[:]).then_inc(pad_kept, 16)

                def keep_xln(b):
                    sp.wait_ge(ln_ready, b.i + 1)
                    sp.dma_start(token_major(xtab, b.i)[:, :, 0:C], xln[b.odd][:]).then_inc(tables_kept[b.odd], 16)

                def keep_route(b):
                    sp.wait_ge(route_ready, b.i + 1)
                    sp.dma_start(token_major(xtab, b.i)[:, :, C:ROW], gates_out[b.odd][:]).then_inc(tables_kept[b.odd], 16)
                    sp.wait_ge(cum_read, b.i + 1)
                    sp.dma_start(cumtab[bass.ds(b.i * (TPB * E), TPB * E), :].rearrange("(t e) n -> e t n", e=E),
                                 cum_sb[b.odd][:].rearrange("e (t n) -> e t n", n=P)).then_inc(tables_kept[b.odd], 16)

                def keep_out(b):
                    sp.wait_ge(out_ready, 2 * b.i + 2)
                    sp.dma_start(token_major(acc, b.i), xout[b.odd][:]).then_inc(out_kept[b.odd], 16)

                keep_xln(Blk(0, 0))
                keep_xln(Blk(0, 1))
                keep_route(Blk(0, 0))

                def turn(b, more):
                    need(sp, out_ready, 2 * (b.i - 1))
                    sp.dma_start(xres[b.odd][:], token_major(src, b.i)).then_inc(xres_in[b.odd], 16)
                    if more >= 2:
                        load_x(b.plus(2))
                    if not isinstance(b.i, int) or b.i > 0:
                        keep_out(b.plus(-1))
                    if more >= 1:
                        keep_route(b.plus(1))
                    if more >= 2:
                        keep_xln(b.plus(2))

                pairs_loop(nc, sp, NBLK, turn)
                keep_out(Blk(NBLK // 2 - 1, 1))
                sp.dma_start(cend_dram, cend[:]).then_inc(pad_kept, 16)
                sp.wait_ge(pad_kept, 16 * 4)
                for b in range(2):
                    sp.wait_ge(tables_kept[b], 48 * (NBLK // 2))
                    sp.wait_ge(out_kept[b], 16 * (NBLK // 2))

            @block.gpsimd
            def _(pool):
                nc.gpsimd.memset(zrow[:], 0.0).then_inc(pads_set, 1)
                nc.gpsimd.memset(brow[:], 1.0e9).then_inc(pads_set, 1)

            @block.tensor
            def _(pe):
                def turn_x(b):
                    pe.wait_ge(ln_ready, b.i + 1)
                    need(pe, logits_read, b.i)
                    need(pe, cum_read, b.i)
                    for c in range(CC):
                        for t in range(TPB):
                            last = pe.transpose(side[c][:, t * P:(t + 1) * P],
                                                xln[b.odd][:, t, c * P:(c + 1) * P], ident[:])
                    last.then_inc(turned, 1)

                def logits(b):
                    pe.wait_ge(xT_ready, b.i + 1)
                    for t in range(TPB):
                        for c in range(CC):
                            last = pe.matmul(side[0][:, t * E:(t + 1) * E], xT[b.odd][:, c, t * P:(t + 1) * P],
                                             wg_sb[:, c, :], start=(c == 0), stop=(c == CC - 1))
                    last.then_inc(logits_ready, 1)

                def ranks(b):
                    pe.wait_ge(route_ready, b.i + 1)
                    for t in range(TPB):
                        last = pe.matmul(side[1][0:E, t * P:BLK], mask[:, t, :], tri[:, t, t * P:BLK],
                                         start=(t == 0), stop=(t == TPB - 1), skip_group_check=True)
                    last.then_inc(cum_ready, 1)

                def up(b, f):
                    need(pe, h_ready, b.i * FC + f - 1)
                    if f == 0:
                        pe.wait_ge(xT_split, b.i + 1)
                    for half, dst in ((0, up1[f % 2]), (1, up2[f % 2])):
                        o = half * F + f * P
                        for c in range(CC):
                            for w, x in ((w1_hi, xT_hi), (w1_hi, xT_lo), (w1_lo, xT_hi)):
                                last = pe.matmul(dst[:], w[:, c, o:o + P], x[b.odd][:, c, :],
                                                 start=(c == 0 and x is xT_hi and w is w1_hi),
                                                 stop=(c == CC - 1 and w is w1_lo))
                    last.then_inc(up_ready, 1)

                def downs(b):
                    for q in range(2):
                        need(pe, out_ready, 2 * b.i + q - 1)
                        for t in range(2 * q, 2 * q + 2):
                            for f in range(FC):
                                pe_ready = b.i * FC + f + 1
                                if t == 0:
                                    pe.wait_ge(h_ready, pe_ready)
                                last = pe.matmul(down[q][:, (t % 2) * C:(t % 2 + 1) * C],
                                                 hT[b.odd][:, f, t * P:(t + 1) * P], w2[:, f, :],
                                                 start=(f == 0), stop=(f == FC - 1))
                        last.then_inc(down_ready, 1)

                pe.wait_ge(first_in, 16 * N_FIRST)
                turn_x(Blk(0, 0))
                logits(Blk(0, 0))
                pe.wait_ge(const_in, 16 * N_CONST)
                pe.wait_ge(set_up, 2)
                ranks(Blk(0, 0))

                def turn(b, more):
                    if more:
                        turn_x(b.plus(1))
                    up(b, 0)
                    if more:
                        logits(b.plus(1))
                    for f in range(1, FC):
                        up(b, f)
                    if more:
                        ranks(b.plus(1))
                    downs(b)

                pairs_loop(nc, pe, NBLK, turn)

            @block.scalar
            def _(act):
                def std_of(b):
                    act.wait_ge(var_ready, b.i + 1)
                    act.activation(std[:], varp[:], ACT.Sqrt).then_inc(std_ready, 1)

                def out_xT(b):
                    act.wait_ge(turned, b.i + 1)
                    act.activation(xT[b.odd][:, 0, :], side[0][:], ACT.Copy)
                    act.activation(xT[b.odd][:, 1, :], side[1][:], ACT.Copy).then_inc(xT_ready, 1)

                def split_xT(b):
                    act.wait_ge(xT_ready, b.i + 1)
                    act.activation(xT_hi[b.odd][:], xT[b.odd][:], ACT.Copy).then_inc(xT_hi_ready, 1)

                def exps(b):
                    act.wait_ge(logits_read, b.i + 1)
                    act.activation(ez[:], zlog[:], ACT.Exp).then_inc(ez_ready, 1)

                def silus(b, f):
                    act.wait_ge(up_ready, b.i * FC + f + 1)
                    need(act, h_ready, b.i * FC + f - 1)
                    act.activation(silu[f % 2][:], up2[f % 2][:], ACT.Silu).then_inc(silu_ready, 1)

                std_of(Blk(0, 0))
                act.wait_ge(first_in, 16 * N_FIRST)
                act.activation(w1_hi[:], w1, ACT.Copy).then_inc(w1_hi_ready, 1)
                out_xT(Blk(0, 0))
                split_xT(Blk(0, 0))
                std_of(Blk(0, 1))
                exps(Blk(0, 0))

                def turn(b, more):
                    if more:
                        out_xT(b.plus(1))
                    silus(b, 0)
                    if more:
                        split_xT(b.plus(1))
                    silus(b, 1)
                    if more:
                        exps(b.plus(1))
                    for f in range(2, FC):
                        silus(b, f)
                    if more >= 2:
                        std_of(b.plus(2))

                pairs_loop(nc, act, NBLK, turn)

            @block.vector
            def _(dve):
                st = Steps(dve, vec)
                st.step(dve.memset(carry[:], 0.0))

                def ln_stats(b):
                    dve.wait_ge(x_in[b.odd], 16 * (b.pair + 1))
                    for t in range(TPB):
                        st.step(dve.bn_stats(stats[:, t, :], xin[b.odd][:, t, :]))
                    st.settle_on(unused[:])
                    for t in range(TPB):
                        st.step(dve.bn_aggr(mv[:, t, :], stats[:, t, :]))
                    st.settle()
                    need(dve, std_ready, b.i)
                    dve.tensor_scalar(varp[:], mv[:, :, 1], EPS, None, ALU.add).then_inc(var_ready, 1)

                def ln_apply(b):
                    dve.wait_ge(std_ready, b.i + 1)
                    rsqrt_refined(dve, st, rstd, varp, std, newton)
                    need(dve, tables_kept[b.odd], 48 * b.pair)
                    need(dve, turned, b.i - 1)
                    for t in range(TPB):
                        last = dve.tensor_scalar(xln[b.odd][:, t, :], xin[b.odd][:, t, :], mv[:, t, 0:1],
                                                 rstd[:, t:t + 1], ALU.subtract, ALU.mult)
                        if t < TPB - 1:
                            st.step(last)
                    last.then_inc(ln_ready, 1)

                def lo_xT(b):
                    dve.wait_ge(xT_hi_ready, b.i + 1)
                    dve.tensor_tensor(xT_lo[b.odd][:], xT[b.odd][:], xT_hi[b.odd][:].bitcast(F32), ALU.subtract)\
                       .then_inc(xT_split, 1)

                def bc(x, n):
                    return x.unsqueeze(2).to_broadcast([P, TPB, n])

                def route_a(b):
                    lg = side[0][:, 0:TPB * E].rearrange("p (t e) -> p t e", t=TPB)
                    dve.wait_ge(logits_ready, b.i + 1)
                    st.step(dve.tensor_reduce(negmax[:], lg, AX.X, ALU.max, negate=True))
                    st.settle()
                    dve.tensor_tensor(zlog[:], lg, bc(negmax[:], E), ALU.add).then_inc(logits_read, 1)

                def route_b(b):
                    dve.wait_ge(ez_ready, b.i + 1)
                    st.step(dve.tensor_reduce(esum[:], ez[:], AX.X, ALU.add))
                    st.settle()
                    st.step(dve.reciprocal(rsum[:], esum[:]))
                    st.settle()
                    st.step(dve.tensor_tensor(gate[:], ez[:], bc(rsum[:], E), ALU.mult))
                    st.settle_on(unused[:])
                    for t in range(TPB):
                        st.step(dve.max(top8[:, t, :], gate[:, t, :]))
                    st.settle()

                def route_c(b):
                    for t in range(TPB):
                        st.step(dve.match_replace(struck[:, t, :], top8[:, t, :], gate[:, t, :], -1.0))
                    st.step(dve.tensor_reduce(tsum[:], top8[:], AX.X, ALU.add))
                    st.settle()
                    need(dve, cum_ready, b.i)
                    st.step(dve.tensor_scalar(mask[:], struck[:], 0.0, None, ALU.is_lt))
                    st.step(dve.tensor_scalar(tclip[:], tsum[:], FLT_EPS, None, ALU.max))
                    st.settle()
                    st.step(dve.reciprocal(trec[:], tclip[:]))
                    st.settle()
                    st.step(dve.tensor_scalar(thalf[:], trec[:], 0.5, None, ALU.mult))
                    st.settle()
                    st.step(dve.tensor_tensor(gscaled[:], gate[:], bc(thalf[:], E), ALU.mult))
                    st.settle()
                    dve.tensor_tensor(gates_out[b.odd][:], gscaled[:], mask[:], ALU.mult).then_inc(route_ready, 1)

                def cum_out(b):
                    dve.wait_ge(cum_ready, b.i + 1)
                    st.settle()
                    st.step(dve.tensor_scalar(cum_sb[b.odd][:], side[1][0:E, :], carry[:], None, ALU.add))
                    st.settle()
                    st.step(dve.tensor_copy(carry[:], cum_sb[b.odd][:, BLK - 1:BLK]))
                    dve.tensor_copy(cend[:, bass.ds(b.i * TPB, TPB)],
                                    cum_sb[b.odd][:, P - 1:BLK:P]).then_inc(cum_read, 1)

                def product(b, f):
                    dve.wait_ge(silu_ready, b.i * FC + f + 1)
                    need(dve, down_ready, 2 * (b.i - 1))
                    dve.tensor_tensor(hT[b.odd][:, f, :], up1[f % 2][:], silu[f % 2][:], ALU.mult)\
                       .then_inc(h_ready, 1)

                def out_sum(b):
                    dve.wait_ge(xres_in[b.odd], 16 * (b.pair + 1))
                    need(dve, out_kept[b.odd], 16 * b.pair)
                    for q in range(2):
                        dve.wait_ge(down_ready, 2 * b.i + q + 1)
                        dve.scalar_tensor_tensor(xout[b.odd][:, 2 * q:2 * q + 2, :],
                                                 down[q][:].rearrange("p (t n) -> p t n", t=2), 0.5,
                                                 xres[b.odd][:, 2 * q:2 * q + 2, :], ALU.mult, ALU.add)\
                           .then_inc(out_ready, 1)

                ln_stats(Blk(0, 0))
                ln_apply(Blk(0, 0))
                ln_stats(Blk(0, 1))
                dve.wait_ge(w1_hi_ready, 1)
                dve.tensor_tensor(w1_lo[:], w1, w1_hi[:].bitcast(F32), ALU.subtract)\
                   .then_inc(set_up, 1)
                route_a(Blk(0, 0))
                dve.wait_ge(const_in, 16 * N_CONST)
                dve.tensor_copy(tri[:], tri_f[:]).then_inc(set_up, 1)
                route_b(Blk(0, 0))
                route_c(Blk(0, 0))
                lo_xT(Blk(0, 0))
                ln_apply(Blk(0, 1))
                cum_out(Blk(0, 0))

                def turn(b, more):
                    product(b, 0)
                    if more:
                        route_a(b.plus(1))
                    product(b, 1)
                    if more:
                        route_b(b.plus(1))
                    product(b, 2)
                    if more:
                        route_c(b.plus(1))
                    product(b, 3)
                    if more:
                        lo_xT(b.plus(1))
                    product(b, 4)
                    product(b, 5)
                    if more >= 2:
                        ln_stats(b.plus(2))
                    if more:
                        cum_out(b.plus(1))
                    if more >= 2:
                        ln_apply(b.plus(2))
                    out_sum(b)

                pairs_loop(nc, dve, NBLK, turn, st)


def ffn_routed(nc, tag, acc, xtab, cumtab, cend_dram, a):
    WE = CC * 2 * F + FC * C
    HF = FC // 2
    CH = GRP + 1
    with ExitStack() as ctx:
        def sb(name, shape, dt=F32):
            return ctx.enter_context(nc.sbuf_tensor(f"{tag}_{name}", shape, dt))

        def sem(name):
            return nc.alloc_semaphore(f"{tag}_{name}")

        def bank(name):
            return ctx.enter_context(nc.psum_tensor(f"{tag}_{name}", [P, 512], F32))

        ident = sb("ident", [P, P])
        slot = sb("slot", [P, CH + 1])
        erow = sb("erow", [P, NG, CH])
        cend_all = sb("cend_all", [P, E, NT])
        cend_tail = sb("cend_tail", [P, NG, NT])
        w = [sb(f"w{k}", [P, WE]) for k in range(GRP)]
        w1 = [x[:, 0:CC * 2 * F].rearrange("p (c f) -> p c f", c=CC) for x in w]
        w2 = [x[:, CC * 2 * F:WE].rearrange("p (f n) -> p f n", f=FC) for x in w]
        unused = sb("unused", [P, 3])
        ended = sb("ended", [P, CH, NT])
        tile_of = sb("tile_of", [P, CH])
        cum_idx = sb("cum_idx", [P, CH], I32)
        cum_rows = sb("cum_rows", [P, CH, P])
        below = sb("below", [P, CH, P])
        count = sb("count", [P, CH])
        token0 = sb("token0", [P, CH])
        pad = sb("pad", [P, CH])
        token = sb("token", [P, CH])
        x_idx = sb("x_idx", [P, CH], I32)
        y_idx = sb("y_idx", [P, GRP], I32)
        yt_idx = sb("yt_idx", [TAIL, GRP], I32)
        x_rows = sb("x_rows", [P, CH, ROW])
        xT = sb("xT", [P, CC, GRP, CAP])
        wy = sb("wy", [P, GRP])
        wyt = sb("wyt", [TAIL, GRP])
        silu = [sb(f"silu{b}", [P, HF * CAP]) for b in range(2)]
        hT = [sb(f"hT{b}", [P, FC, CAP]) for b in range(2)]
        yT = sb("yT", [P, CC, CAP])
        y = sb("y", [P, GRP, C])
        yt = sb("yt", [TAIL, GRP, C])

        up1 = [bank(f"up1_{b}") for b in range(2)]
        up2 = [bank(f"up2_{b}") for b in range(2)]
        down = bank("down")
        back = bank("back")
        turn_x = [bank(f"turn{c}") for c in range(CC)]

        const_in = sem("const_in")
        cend_in = sem("cend_in")
        w_in = [sem(f"w_in{k}") for k in range(GRP)]
        vec = sem("vec")
        unused_set = sem("unused_set")
        held = sem("held")
        cum_idx_ready = sem("cum_idx_ready")
        cum_in = sem("cum_in")
        token_ready = sem("token_ready")
        x_idx_ready = sem("x_idx_ready")
        y_idx_ready = sem("y_idx_ready")
        x_rows_in = sem("x_rows_in")
        turned = sem("turned")
        xT_ready = sem("xT_ready")
        wy_ready = sem("wy_ready")
        up_ready = sem("up_ready")
        silu_ready = sem("silu_ready")
        h_ready = sem("h_ready")
        down_ready = sem("down_ready")
        yT_ready = sem("yT_ready")
        back_ready = sem("back_ready")
        y_ready = sem("y_ready")
        y_added = sem("y_added")
        N_CONST = 4 + GRP

        def groups_loop(eng, body, steps=None):
            start = steps.n if steps else 0
            body(0, 2)
            per = steps.n - start if steps else 0
            with eng.Fori(1, NG - 2) as g:
                if steps:
                    steps.loop(g - 1, per)
                body(g, 2)
            if steps:
                steps.end_loop(NG - 3)
            body(NG - 2, 1)
            body(NG - 1, 0)

        with nc.Block() as block:

            @block.sync
            def _(sp):
                sp.dma_start(slot[:], a["slot"]).then_inc(const_in, 16)
                sp.dma_start(erow[:], a["erow"]).then_inc(const_in, 16)
                sp.dma_start(cend_all[:, 0:2 * GRP, :],
                             cend_dram[0:2 * GRP, :].unsqueeze(0).to_broadcast([P, 2 * GRP, NT])).then_inc(const_in, 16)
                for k in range(GRP):
                    rows = cend_dram.rearrange("(g k) t -> k g t", k=GRP)[k].unsqueeze(0)
                    sp.dma_start(cend_tail[TAIL * k:TAIL * (k + 1), :, :],
                                 rows.to_broadcast([TAIL, NG, NT])).then_inc(const_in, 16)
                sp.dma_start(ident[:], a["ident"]).then_inc(const_in, 16)

                def turn(g, more):
                    for k in range(GRP):
                        if isinstance(g, int) and g == 0 and k in (1, 2):
                            sp.wait_ge(cum_in, 16 * CH * k)
                        need(sp, down_ready, GRP * (g - 1) + k + 1)
                        sp.dma_start(w[k][:], a["experts"][bass.ds(g * GRP + k, 1), :, :].squeeze(0))\
                          .then_inc(w_in[k], 16)
                    if isinstance(g, int) and g == 0:
                        sp.dma_start(cend_all[:, 2 * GRP:E, :],
                                     cend_dram[2 * GRP:E, :].unsqueeze(0).to_broadcast([P, E - 2 * GRP, NT]))\
                            .then_inc(cend_in, 16)

                groups_loop(sp, turn)

            @block.gpsimd
            def _(pool):
                st = Steps(pool, held)

                def settle():
                    st.settle()
                    st.step(pool.tensor_tensor(unused[:, 0:1], unused[:, 1:2], unused[:, 2:3], ALU.add))

                pool.memset(unused[:], 0.0).then_inc(unused_set, 1)
                pool.wait_ge(unused_set, 1)

                def gather_cum(g):
                    pool.wait_ge(cum_idx_ready, g + 1)
                    need(pool, token_ready, g)
                    settle()
                    for j in range(CH):
                        pool.indirect_dma_start(cum_rows[:, j, :], None, cumtab,
                                                bass.IndirectOffsetOnAxis(ap=cum_idx[:, j:j + 1], axis=0))\
                            .then_inc(cum_in, 16)

                def gather_x(g):
                    pool.wait_ge(x_idx_ready, g + 1)
                    need(pool, turned, 2 * g)
                    need(pool, wy_ready, g)
                    settle()
                    for j in range(CH):
                        pool.indirect_dma_start(x_rows[:, j, :], None, xtab,
                                                bass.IndirectOffsetOnAxis(ap=x_idx[:, j:j + 1], axis=0))\
                            .then_inc(x_rows_in, 16)

                def add_y(g, k):
                    pool.wait_ge(y_ready, g * GRP + k + 1)
                    if k == 0:
                        pool.wait_ge(y_idx_ready, g + 1)
                    need(pool, y_added, 32 * (g * GRP + k))
                    settle()
                    for idx, rows in ((y_idx, y), (yt_idx, yt)):
                        pool.indirect_dma_start(acc, bass.IndirectOffsetOnAxis(ap=idx[:, k:k + 1], axis=0),
                                                rows[:, k, :], None, compute_op=ALU.add).then_inc(y_added, 16)

                gather_cum(0)
                gather_x(0)
                gather_cum(1)

                def turn(g, more):
                    if more >= 1:
                        gather_x(g + 1)
                    if more >= 2:
                        gather_cum(g + 2)
                    for k in range(GRP):
                        add_y(g, k)

                groups_loop(pool, turn, st)
                pool.wait_ge(y_added, 32 * E)

            @block.tensor
            def _(pe):
                def turn_full(g):
                    pe.wait_ge(x_rows_in, 16 * CH * (g + 1))
                    need(pe, xT_ready, 2 * g)
                    for c in range(CC):
                        for k in range(GRP):
                            last = pe.transpose(turn_x[c][:, k * P:(k + 1) * P],
                                                x_rows[:, k, c * P:(c + 1) * P], ident[:])
                    last.then_inc(turned, 1)

                def turn_tail(g):
                    pe.wait_ge(xT_ready, 2 * g + 1)
                    for c in range(CC):
                        last = pe.transpose(turn_x[0][:, c * P:(c + 1) * P],
                                            x_rows[:, GRP, c * P:(c + 1) * P], ident[:])
                    last.then_inc(turned, 1)

                def up(g, k, s):
                    x = g * GRP + k
                    if s == 0:
                        pe.wait_ge(w_in[k], 16 * (g + 1))
                        if k == 0:
                            pe.wait_ge(xT_ready, 2 * g + 2)
                    need(pe, h_ready, 2 * x + s - 1)
                    for half, dst in ((0, up1[s]), (1, up2[s])):
                        for j in range(HF):
                            o = half * F + (s * HF + j) * P
                            for c in range(CC):
                                last = pe.matmul(dst[:, j * CAP:(j + 1) * CAP], w1[k][:, c, o:o + P],
                                                 xT[:, c, k, :], start=(c == 0), stop=(c == CC - 1))
                    last.then_inc(up_ready, 1)

                def downs(g, k):
                    x = g * GRP + k
                    need(pe, yT_ready, x)
                    pe.wait_ge(h_ready, 2 * x + 2)
                    for c in range(CC):
                        for f in range(FC):
                            last = pe.matmul(down[:, c * CAP:(c + 1) * CAP], w2[k][:, f, c * P:(c + 1) * P],
                                             hT[k % 2][:, f, :], start=(f == 0), stop=(f == FC - 1))
                    last.then_inc(down_ready, 1)

                def backs(g, k):
                    x = g * GRP + k
                    pe.wait_ge(yT_ready, x + 1)
                    need(pe, y_ready, x)
                    for c in range(CC):
                        pe.transpose(back[:, c * P:(c + 1) * P], yT[:, c, 0:P], ident[:])
                        last = pe.transpose(back[0:TAIL, C + c * P:C + (c + 1) * P], yT[:, c, P:CAP], ident[:])
                    last.then_inc(back_ready, 1)

                pe.wait_ge(const_in, 16 * N_CONST)
                turn_full(0)
                turn_tail(0)

                def turn(g, more):
                    up(g, 0, 0)
                    up(g, 0, 1)
                    for k in range(1, GRP):
                        up(g, k, 0)
                        downs(g, k - 1)
                        up(g, k, 1)
                        backs(g, k - 1)
                    if more:
                        turn_full(g + 1)
                    downs(g, GRP - 1)
                    if more:
                        turn_tail(g + 1)
                    backs(g, GRP - 1)

                groups_loop(pe, turn)

            @block.scalar
            def _(act):
                def out_xT(g):
                    act.wait_ge(turned, 2 * g + 1)
                    for c in range(CC):
                        last = act.activation(xT[:, c, :, 0:P], turn_x[c][:].rearrange("p (k n) -> p k n", k=GRP),
                                              ACT.Copy)
                    last.then_inc(xT_ready, 1)

                def out_xT_tail(g):
                    act.wait_ge(turned, 2 * g + 2)
                    for c in range(CC):
                        last = act.activation(xT[:, c, :, P:CAP],
                                              turn_x[0][:, c * P:(c + 1) * P].rearrange("p (k n) -> p k n", k=GRP),
                                              ACT.Copy)
                    last.then_inc(xT_ready, 1)

                def silus(g, k, s):
                    x = g * GRP + k
                    act.wait_ge(up_ready, 2 * x + s + 1)
                    need(act, h_ready, 2 * x + s - 1)
                    act.activation(silu[s][:], up2[s][:, 0:HF * CAP], ACT.Silu).then_inc(silu_ready, 1)

                def out_yT(g, k):
                    x = g * GRP + k
                    act.wait_ge(down_ready, x + 1)
                    need(act, back_ready, x)
                    act.activation(yT[:], down[:, 0:CC * CAP].rearrange("p (c n) -> p c n", c=CC), ACT.Copy)\
                       .then_inc(yT_ready, 1)

                out_xT(0)
                out_xT_tail(0)

                def turn(g, more):
                    silus(g, 0, 0)
                    silus(g, 0, 1)
                    for k in range(1, GRP):
                        silus(g, k, 0)
                        out_yT(g, k - 1)
                        silus(g, k, 1)
                    if more:
                        out_xT(g + 1)
                    out_yT(g, GRP - 1)
                    if more:
                        out_xT_tail(g + 1)

                groups_loop(act, turn)

            @block.vector
            def _(dve):
                st = Steps(dve, vec)

                def tiles_of(g):
                    need(dve, token_ready, g)
                    st.step(dve.tensor_scalar(ended[:, 0:GRP, :], cend_all[:, bass.ds(g * GRP, GRP), :],
                                              slot[:, 0:1], None, ALU.is_le))
                    st.step(dve.tensor_scalar(ended[:, GRP, :], cend_tail[:, bass.ds(g, 1), :].rearrange("p a t -> p (a t)"),
                                              slot[:, GRP:GRP + 1], None, ALU.is_le))
                    st.settle()
                    st.step(dve.tensor_reduce(tile_of[:], ended[:], AX.X, ALU.add))
                    st.settle()
                    need(dve, cum_in, 16 * CH * g)
                    dve.scalar_tensor_tensor(cum_idx[:], tile_of[:], float(E),
                                             erow[:, bass.ds(g, 1), :].rearrange("p a j -> p (a j)"),
                                             ALU.mult, ALU.add).then_inc(cum_idx_ready, 1)

                def tokens_of(g):
                    dve.wait_ge(cum_in, 16 * CH * (g + 1))
                    st.step(dve.tensor_tensor(below[:], cum_rows[:],
                                              slot[:, 0:CH].unsqueeze(2).to_broadcast([P, CH, P]), ALU.is_le))
                    st.settle()
                    st.step(dve.tensor_reduce(count[:], below[:], AX.X, ALU.add))
                    st.step(dve.tensor_scalar(pad[:], tile_of[:], float(NT), slot[:, CH:CH + 1], ALU.is_ge, ALU.mult))
                    st.settle()
                    st.step(dve.scalar_tensor_tensor(token0[:], tile_of[:], float(P), count[:], ALU.mult, ALU.add))
                    st.settle()
                    need(dve, x_idx_ready, g)
                    dve.tensor_tensor(token[:], token0[:], pad[:], ALU.add).then_inc(token_ready, 1)

                def x_indices(g):
                    dve.wait_ge(token_ready, g + 1)
                    need(dve, x_rows_in, 16 * CH * g)
                    if not isinstance(g, int) or g > 0:
                        dve.wait_ge(y_idx_ready, g)
                    dve.tensor_copy(x_idx[:], token[:]).then_inc(x_idx_ready, 1)

                def y_indices(g):
                    dve.wait_ge(x_idx_ready, g + 1)
                    need(dve, y_added, 32 * GRP * g)
                    st.step(dve.tensor_copy(y_idx[:], x_idx[:, 0:GRP]))
                    for k in range(GRP):
                        last = dve.tensor_copy(yt_idx[:, k:k + 1], x_idx[TAIL * k:TAIL * (k + 1), GRP:CH])
                        if k < GRP - 1:
                            st.step(last)
                    last.then_inc(y_idx_ready, 1)

                def gate_weights(g):
                    dve.wait_ge(x_rows_in, 16 * CH * (g + 1))
                    need(dve, y_ready, GRP * g)
                    for k in range(GRP):
                        col = bass.ds(g * GRP + (C + k), 1)
                        st.step(dve.tensor_copy(wy[:, k:k + 1], x_rows[:, k, col]))
                        last = dve.tensor_copy(wyt[:, k:k + 1], x_rows[TAIL * k:TAIL * (k + 1), GRP, col])
                        if k < GRP - 1:
                            st.step(last)
                    last.then_inc(wy_ready, 1)

                def product(g, k, s):
                    x = g * GRP + k
                    dve.wait_ge(silu_ready, 2 * x + s + 1)
                    need(dve, down_ready, x - 1)
                    dve.tensor_tensor(hT[k % 2][:, s * HF:(s + 1) * HF, :],
                                      up1[s][:, 0:HF * CAP].rearrange("p (f n) -> p f n", f=HF),
                                      silu[s][:].rearrange("p (f n) -> p f n", f=HF), ALU.mult).then_inc(h_ready, 1)

                def weigh(g, k):
                    x = g * GRP + k
                    dve.wait_ge(back_ready, x + 1)
                    if k == 0:
                        dve.wait_ge(wy_ready, g + 1)
                    need(dve, y_added, 32 * (x - GRP + 1))
                    st.step(dve.tensor_scalar(y[:, k, :], back[:, 0:C], wy[:, k:k + 1], None, ALU.mult))
                    dve.tensor_scalar(yt[:, k, :], back[0:TAIL, C:2 * C], wyt[:, k:k + 1], None, ALU.mult)\
                       .then_inc(y_ready, 1)

                dve.wait_ge(const_in, 16 * N_CONST)
                tiles_of(0)
                tokens_of(0)
                x_indices(0)
                tiles_of(1)
                tokens_of(1)

                def turn(g, more):
                    product(g, 0, 0)
                    product(g, 0, 1)
                    y_indices(g)
                    gate_weights(g)
                    if more >= 1:
                        x_indices(g + 1)
                    if isinstance(g, int) and g == 0:
                        dve.wait_ge(cend_in, 16)
                    if more >= 2:
                        tiles_of(g + 2)
                    for k in range(1, GRP):
                        product(g, k, 0)
                        product(g, k, 1)
                        weigh(g, k - 1)
                        if k == 2 and more >= 2:
                            tokens_of(g + 2)
                    weigh(g, GRP - 1)

                groups_loop(dve, turn, st)


HC = NH // 4
STACK = 3 * L
SHIFT = STACK + 2

CHUNKS = (3, 0, 1, 2)
GROUPS = ((0, 1), (2,), (3,))
BACK = [("o", c) for c in range(HC)] + [("yT", c) for c in range(CC)] + [("proj", u) for u in range(2)]
BY_SCALAR = ("xT", "yT")
SLOTS = [[("o", 0), ("xT", 0), ("o", 1), ("xT", 1)],
         [("o", 2), ("q", 0), ("q", 1), ("o", 3)],
         [("k", 0), ("k", 1), ("latq", 3), ("latq_s", 3)],
         [("yT", 0), ("latk", 3), ("latk_s", 3), ("yT", 1)],
         [("proj", 0), ("qk", 3), ("proj", 1)],
         [("latq", 0), ("latq_s", 0), ("latk", 0), ("latk_s", 0)],
         [("latq", 1), ("qk", 0), ("latq_s", 1)],
         [("latk", 1), ("latk_s", 1), ("max", 12)],
         [("latq", 2), ("qk", 1), ("latq_s", 2), ("max", 13)],
         [("latk", 2), ("latk_s", 2), ("max", 14)],
         [("qk", 2), ("max", 15)],
         [("max", 0), ("max", 1)],
         [("max", 2), ("max", 3)],
         [("max", 4), ("max", 5)],
         [("max", 6), ("max", 7)],
         [("max", 8), ("max", 9)],
         [("max", 10), ("max", 11)],
         [("v", 0), ("v", 1)]]


def mixed(n_own, n_taken):
    steps = [((n + 1.0) / n_own, True, n) for n in range(n_own)]
    steps += [((n + 0.9) / n_taken, False, n) for n in range(n_taken)]
    return [(own, n) for _, own, n in sorted(steps)]


def read_before(items, n, scalar):
    return sum((name in BY_SCALAR) == scalar for name, _ in items[:n])


def attention(nc, tag, src, dst, a):
    scale = float(np.float32(L ** -0.5))
    FR = mybir.dt.float32r
    with ExitStack() as ctx:
        def sb(name, shape, dt=F32):
            return ctx.enter_context(nc.sbuf_tensor(f"{tag}_{name}", shape, dt))

        def sem(name):
            return nc.alloc_semaphore(f"{tag}_{name}")

        def bank(name):
            return ctx.enter_context(nc.psum_tensor(f"{tag}_{name}", [P, 512], F32))

        ident = sb("ident", [P, P])
        ident_b = sb("ident_b", [P, P], BF16)
        masks = sb("masks", [P, 2, P], BF16)
        wqk_in = sb("wqk_in", [P, CC, 2 * C])
        latq_hi = sb("latq_hi", [P, 2, 2, P], FR)
        latq_lo = sb("latq_lo", [P, 2, 2, P], FR)
        latk_hi = sb("latk_hi", [P, 2, 2, P], FR)
        latk_lo = sb("latk_lo", [P, 2, 2, P], FR)
        qk_w = sb("qk_w", [P, P])
        cols = sb("cols", [P, 9])
        cos = sb("cos", [P, BLK])
        sin = sb("sin", [P, BLK])
        kv8 = sb("kv8", [L, P])
        l2o8 = sb("l2o8", [L, P])
        bmask = sb("bmask", [P, P])
        bv = sb("bv", [P, 2])
        kvb = sb("kvb", [L, 1])
        l2ob = sb("l2ob", [P, C])
        at8 = sb("at8", [P, P])
        wvp = sb("wvp", [P, CC, C])
        bvb = sb("bvb", [P, 2, P])
        kvbb = sb("kvbb", [L, P])
        vbias = sb("vbias", [P, C])
        wp = sb("wp", [P, CC, C])
        pbias = sb("pbias", [P, C])
        xin = sb("xin", [P, TPB, C])
        xres = sb("xres", [P, TPB, C])
        xln = sb("xln", [P, TPB, C])
        xT = sb("xT", [P, CC, BLK])
        qT_hi = sb("qT_hi", [P, CC, BLK], FR)
        qT_lo = sb("qT_lo", [P, CC, BLK], FR)
        kT_hi = sb("kT_hi", [P, CC, BLK], FR)
        kT_lo = sb("kT_lo", [P, CC, BLK], FR)
        rot = {x: sb(f"rot_{x}", [P, BLK]) for x in ("latq", "latq_s", "latk", "latk_s")}
        latq_w = rot["latq"][:].rearrange("p (a b n) -> p a b n", a=2, b=2)
        latk_w = rot["latk"][:].rearrange("p (a b n) -> p a b n", a=2, b=2)
        wv = rot["latq_s"][:].rearrange("p (g n) -> p g n", g=2)
        masks_f = rot["latk_s"][:, 0:2 * P].rearrange("p (m n) -> p m n", m=2)
        rotq = sb("rotq", [P, BLK])
        rotk = sb("rotk", [P, BLK])
        K_HI, K_LO, Q_HI, Q_LO = range(4)
        parts = [sb(f"parts{b}", [P, 4, BLK], FR) for b in range(2)]
        stacks = sb("stacks", [SHIFT, NH - 4, 2, BLK], FR)
        stacks3 = [sb(f"stacks3_{b}", [SHIFT, 4, 2, BLK], FR) for b in range(2)]
        v = sb("v", [P, TPB, NH, L])
        negmax = sb("negmax", [P, TPB, NH])
        m_hi = sb("m_hi", [NH, BLK], FR)
        m_lo = sb("m_lo", [NH, BLK], FR)
        PW = BLK + (BLK - P) + (BLK - 2 * P) + P
        PO = [0, BLK, BLK + BLK - P, PW - P]
        prob = [sb(f"prob{b}", [P, PW]) for b in range(2)]
        o_sb = sb("o", [P, HC, BLK])
        orec = sb("orec", [P, TPB, 4])
        ytok = sb("ytok", [P, TPB, C])
        yT = sb("yT", [P, CC, BLK])
        stats = sb("stats", [P, TPB, 6])
        mv = sb("mv", [P, TPB, 2])
        varp = sb("varp", [P, TPB])
        std = sb("std", [P, TPB])
        rstd = sb("rstd", [P, TPB])
        newton = sb("newton", [P, TPB])
        cell = sb("cell", [P, 3])
        unused = sb("unused", [P, 1])

        work = [bank(f"work{b}") for b in range(2)]
        smax = [bank(f"smax{b}") for b in range(2)]
        score = [bank(f"score{b}") for b in range(3)]
        obank = bank("obank")

        const_in = sem("const_in")
        set_up = sem("set_up")
        set_mm = sem("set_mm")
        x_in = sem("x_in")
        xres_in = sem("xres_in")
        stack_in = [sem(f"stack_in{c}") for c in range(HC)]
        shift_in = sem("shift_in")
        out_kept = sem("out_kept")
        vec = sem("vec")
        var_ready = sem("var_ready")
        std_ready = sem("std_ready")
        held = sem("held")
        rstd_ready = sem("rstd_ready")
        ln_ready = sem("ln_ready")
        front_ready = sem("front_ready")
        front_act = sem("front_act")
        front_dve = sem("front_dve")
        back_ready = sem("back_ready")
        back_act = sem("back_act")
        back_dve = sem("back_dve")
        split_ready = sem("split_ready")
        rotq_ready = sem("rotq_ready")
        rotk_ready = sem("rotk_ready")
        hi_ready = sem("hi_ready")
        qk_hi_ready = sem("qk_hi_ready")
        smax_ready = sem("smax_ready")
        smax_read = sem("smax_read")
        neg_ready = sem("neg_ready")
        m_ready = sem("m_ready")
        score_ready = sem("score_ready")
        exp_ready = sem("exp_ready")
        pv_ready = sem("pv_ready")
        o_out = sem("o_out")
        xres_ready = sem("xres_ready")
        N_CONST = 17
        items = [x for slot in SLOTS for x in slot if x[0] != "max"]
        front = [x for x in items if x not in BACK]
        assert len(items) % 2 == 0 and [x for x in items if x in BACK] == BACK
        assert items[-2:] == front[-2:] and not any(name in BY_SCALAR for name, _ in items[-2:])
        NFA, NFD = read_before(front, len(front), True), read_before(front, len(front), False)
        NBA, NBD = read_before(BACK, len(BACK), True), read_before(BACK, len(BACK), False)

        def slot_items(k, with_front, with_back):
            return [x for x in SLOTS[k] if x[0] != "max" and (with_back if x in BACK else with_front)]

        def slot_heads(k):
            return [h for name, h in SLOTS[k] if name == "max"]

        def slot_order(k, with_front, with_back):
            here = slot_items(k, with_front, with_back)
            groups = [("max", (h, g)) for h in slot_heads(k) if with_front for g in range(len(GROUPS))]
            both = [x for pair in zip(here, groups) for x in pair]
            return both + here[len(groups):] + groups[len(here):]

        def bank_of(item):
            return work[items.index(item) % 2]

        def before(item, with_front, with_back):
            at = items.index(item)
            earlier = [x for x in items[at % 2:at:2] if (with_back if x in BACK else with_front)]
            return earlier[-1] if earlier else None

        def wait_ready(eng, i, item):
            if item in BACK:
                eng.wait_ge(back_ready, len(BACK) * i + BACK.index(item) + 1)
            else:
                eng.wait_ge(front_ready, len(front) * i + front.index(item) + 1)

        def taken_by(item):
            scalar = item[0] in BY_SCALAR
            if item in BACK:
                return (back_act, NBA, read_before(BACK, BACK.index(item) + 1, True)) if scalar else \
                       (back_dve, NBD, read_before(BACK, BACK.index(item) + 1, False))
            return (front_act, NFA, read_before(front, front.index(item) + 1, True)) if scalar else \
                   (front_dve, NFD, read_before(front, front.index(item) + 1, False))

        def wait_taken(eng, i, item):
            s, per, place = taken_by(item)
            eng.wait_ge(s, per * i + place)

        max_order = [h for slot in SLOTS for name, h in slot if name == "max"]
        MAX_AT = {h: n for n, h in enumerate(max_order)}

        assert len(GROUPS) * NH % 2 == 0

        def group_tiles(g):
            return [(t, sum((x + 1) * P for x in GROUPS[g] if x < t)) for t in GROUPS[g]]

        def smax_bank(h, g):
            return smax[(len(GROUPS) * MAX_AT[h] + g) % 2]

        def stacked(b, h):
            return stacks[:, h, :, :] if h < NH - 4 else stacks3[b.odd][:, h - (NH - 4), :, :]

        def turns_of(c):
            at = CHUNKS.index(c)
            return at % 2, CHUNKS[at - 2]

        with nc.Block() as block:

            @block.sync
            def _(sp):
                def load_x(i):
                    need(sp, ln_ready, i)
                    sp.dma_start(xin[:], token_major(src, i)).then_inc(x_in, 16)

                load_x(0)
                n = 0
                for dst_, s in ((ident[:], a["ident"]), (masks_f, a["masks"]), (wqk_in[:], a["wqkin"]),
                                (latq_w, a["latq"]), (latk_w, a["latk"]), (qk_w[:], a["qkw"]),
                                (cols[:], a["cols"]), (cos[:], a["cos"]), (sin[:], a["sin"]),
                                (kv8[:], a["kv8"]), (l2o8[:], a["l2o8"]), (bmask[:], a["bmask"]),
                                (wv, a["wv"]), (bv[:], a["bv"]), (kvb[:], a["kvb"]), (wp[:], a["wp"])):
                    sp.dma_start(dst_, s).then_inc(const_in, 16)
                    n += 1
                sp.dma_start(l2ob[:], a["l2ob"].unsqueeze(0).to_broadcast([P, C])).then_inc(const_in, 16)
                sp.dma_start(pbias[:], a["pbias"].unsqueeze(0).to_broadcast([P, C])).then_inc(const_in, 16)
                assert n + 2 == N_CONST + 1

                def stack(b, c):
                    own, _ = turns_of(c)
                    sp.wait_ge(split_ready, HC * b.i + CHUNKS.index(c) + 1)
                    need(sp, score_ready, 3 * (NH * (b.i - (2 if c == 3 else 1)) + 4 * c + 4))
                    for h in range(4):
                        rows = slice(L * h, L * (h + 1))
                        for r, (k_part, q_part) in enumerate(((K_HI, Q_HI), (K_LO, Q_HI), (K_HI, Q_LO))):
                            sp.dma_start(stacked(b, 4 * c + h)[L * r:L * (r + 1), :, :].bitcast(F32),
                                         parts[own][rows, k_part:q_part + 1:q_part - k_part, :].bitcast(F32))\
                                .then_inc(stack_in[c], 16)

                def shift(b):
                    sp.wait_ge(m_ready, b.i + 1)
                    for r, part in ((STACK, m_hi), (STACK + 1, m_lo)):
                        sp.dma_start(stacks[r:r + 1, :, 1, :].bitcast(F32), part[0:NH - 4, :].bitcast(F32))\
                            .then_inc(shift_in, 16)
                        sp.dma_start(stacks3[b.odd][r:r + 1, :, 1, :].bitcast(F32), part[NH - 4:NH, :].bitcast(F32))\
                            .then_inc(shift_in, 16)

                def keep_out(i):
                    sp.wait_ge(back_dve, NBD * (i + 1))
                    sp.dma_start(token_major(dst, i), xres[:]).then_inc(out_kept, 16)

                load_x(1)
                for c in CHUNKS:
                    stack(Blk(0, 0), c)
                shift(Blk(0, 0))

                def turn(b, more):
                    i = b.i
                    if more >= 2:
                        load_x(i + 2)
                    if more:
                        stack(b.plus(1), CHUNKS[0])
                    if not isinstance(i, int) or i > 0:
                        keep_out(i - 1)
                    need(sp, out_kept, 16 * i)
                    sp.dma_start(xres[:], token_major(src, i)).then_inc(xres_in, 16)
                    if more:
                        for c in CHUNKS[1:]:
                            stack(b.plus(1), c)
                        shift(b.plus(1))

                pairs_loop(nc, sp, BATCH, turn)
                keep_out(BATCH - 1)
                sp.wait_ge(out_kept, 16 * BATCH)

            @block.tensor
            def _(pe):
                def to_bank(i, item, with_front, with_back):
                    turn_i = i + 1 if item in BACK else i - 1
                    x = before(item, with_front, with_back)
                    if x:
                        wait_taken(pe, turn_i + (-1 if x in BACK else 1), x)
                    else:
                        need(pe, front_dve, NFD * (turn_i + 1) - 1 + items.index(item) % 2)
                    return bank_of(item)

                def front_item(i, item, with_back):
                    name, c = item
                    if name == "xT" and c == 0:
                        pe.wait_ge(ln_ready, i + 1)
                    if (name, c) == ("q", 0):
                        wait_taken(pe, i, ("xT", CC - 1))
                    if (name, c) == ("latq", CHUNKS[0]):
                        wait_taken(pe, i, ("q", CC - 1))
                    if (name, c) == ("latk", CHUNKS[0]):
                        wait_taken(pe, i, ("k", CC - 1))
                    if name == "qk":
                        pe.wait_ge(rotq_ready, HC * i + CHUNKS.index(c) + 1)
                    w = to_bank(i, item, True, with_back)
                    if name == "xT":
                        for t in range(TPB):
                            last = pe.transpose(w[:, t * P:(t + 1) * P], xln[:, t, c * P:(c + 1) * P], ident[:])
                    elif name in ("q", "k"):
                        o = (C if name == "k" else 0) + c * P
                        for h in range(CC):
                            last = pe.matmul(w[:], wqk_in[:, h, o:o + P], xT[:, h, :],
                                             start=(h == 0), stop=(h == CC - 1))
                    elif name == "v":
                        for t in range(2):
                            tok = (2 * c + t) * P
                            for h in range(CC):
                                last = pe.matmul(w[:, t * C:(t + 1) * C], xT[:, h, tok:tok + P], wvp[:, h, :],
                                                 start=(h == 0), stop=(h == CC - 1))
                    elif name == "qk":
                        last = pe.matmul(w[:], qk_w[:], rotq[:], start=True, stop=True)
                    else:
                        w_hi, w_lo, x_hi, x_lo = (latq_hi, latq_lo, qT_hi, qT_lo) if name[3] == "q" else \
                                                 (latk_hi, latk_lo, kT_hi, kT_lo)
                        for n, (lw, x) in enumerate(((w_hi, x_hi), (w_hi, x_lo), (w_lo, x_hi))):
                            last = pe.matmul(w[:], lw[:, c % 2, int(name.endswith("_s")), :], x[:, c // 2, :],
                                             start=(n == 0), stop=(n == 2))
                    last.then_inc(front_ready, 1)

                def max_group(b, h, g):
                    if h % 4 == 0 and g == 0:
                        pe.wait_ge(stack_in[h // 4], 16 * 12 * (b.i + 1))
                    if h == 4 * CHUNKS[0] and g == 0:
                        need(pe, m_ready, b.i)
                    need(pe, smax_read, len(GROUPS) * (NH * b.i + MAX_AT[h]) + g - 1)
                    s, st_ = smax_bank(h, g), stacked(b, h)
                    for t, o in group_tiles(g):
                        pe.matmul(s[:, o:o + (t + 1) * P], st_[0:STACK, 1, t * P:(t + 1) * P],
                                  st_[0:STACK, 0, 0:(t + 1) * P], start=True, stop=False)
                        last = pe.matmul(s[:, o + t * P:o + (t + 1) * P], ident_b[:], masks[:, 0, :],
                                         start=False, stop=True)
                    last.then_inc(smax_ready, 1)

                def turn_maxima(i):
                    pe.wait_ge(smax_read, len(GROUPS) * NH * (i + 1))
                    for t in range(TPB):
                        last = pe.transpose(smax[0][0:NH, t * P:(t + 1) * P], negmax[:, t, :], ident[:])
                    last.then_inc(neg_ready, 1)

                def scores(b, h, kt):
                    x = NH * b.i + h
                    if h == 0 and kt == 0:
                        pe.wait_ge(shift_in, 64 * (b.i + 1))
                    st_ = stacked(b, h)
                    s, o = (score[kt], 0) if kt < 3 else (score[2], BLK - 2 * P)
                    if kt < 3:
                        need(pe, exp_ready, 3 * (x - 1) + kt + 1)
                    pe.matmul(s[:, o:o + BLK - kt * P], st_[:, 0, kt * P:(kt + 1) * P], st_[:, 1, kt * P:BLK],
                              start=True, stop=False)
                    last = pe.matmul(s[:, o:o + P], ident_b[:], masks[:, 1, :], start=False, stop=True)
                    if kt != 2:
                        last.then_inc(score_ready, 1)

                def weighted(i, h, kt):
                    x = NH * i + h
                    if kt < 3:
                        pe.wait_ge(exp_ready, 3 * x + kt + 1)
                    if kt == 0:
                        if h == 0:
                            wait_taken(pe, i, ("v", 1))
                            need(pe, o_out, HC * i)
                        elif h % 4 == 0:
                            pe.wait_ge(o_out, HC * i + h // 4)
                    q = L * (h % 4)
                    last = pe.matmul(obank[q:q + L, kt * P:BLK], v[:, kt, h, :],
                                     prob[h % 2][:, PO[kt]:PO[kt] + BLK - kt * P],
                                     start=(kt == 0), stop=(kt == TPB - 1))
                    if kt == TPB - 1:
                        last.then_inc(pv_ready, 1)

                def back_item(i, item, w):
                    name, c = item
                    if name == "o":
                        pe.wait_ge(o_out, HC * i + c + 1)
                        for t in range(TPB):
                            last = pe.transpose(w[:, t * P:(t + 1) * P], o_sb[:, c, t * P:(t + 1) * P], ident[:])
                    elif name == "yT":
                        if c == 0:
                            wait_taken(pe, i, ("o", HC - 1))
                        for t in range(TPB):
                            last = pe.transpose(w[:, t * P:(t + 1) * P], ytok[:, t, c * P:(c + 1) * P], ident[:])
                    else:
                        if c == 0:
                            wait_taken(pe, i, ("yT", CC - 1))
                        for t in range(2):
                            tok = (2 * c + t) * P
                            for h in range(CC):
                                last = pe.matmul(w[:, t * C:(t + 1) * C], yT[:, h, tok:tok + P], wp[:, h, :],
                                                 start=(h == 0), stop=(h == CC - 1))
                    last.then_inc(back_ready, 1)

                pe.wait_ge(const_in, 16 * (N_CONST + 1))
                pe.matmul(work[0][:, 0:P], kv8[:], l2o8[:], start=True, stop=True).then_inc(set_mm, 1)
                pe.wait_ge(set_up, 1)
                for h in range(CC):
                    for g in range(2):
                        pe.matmul(work[1][:, h * C + g * P:h * C + (g + 1) * P], wv[:, g, h * P:(h + 1) * P],
                                  at8[:], start=True, stop=True)
                for g in range(2):
                    pe.matmul(score[0][:, g * P:(g + 1) * P], bvb[:, g, :], at8[:], start=True, stop=False)
                    last = pe.matmul(score[0][:, g * P:(g + 1) * P], kvbb[:], l2o8[:], start=False, stop=True)
                last.then_inc(set_mm, 1)
                pe.wait_ge(set_up, 2)

                for k in range(len(SLOTS)):
                    for x in slot_order(k, True, False):
                        if x[0] == "max":
                            max_group(Blk(0, 0), *x[1])
                        else:
                            front_item(0, x, False)
                turn_maxima(0)
                pe.wait_ge(held, 5)

                def turn(b, more):
                    i = b.i
                    with_front, with_back = more > 0, not isinstance(i, int) or i > 0

                    def banked(item):
                        if item in BACK:
                            back_item(i - 1, item, to_bank(i - 1, item, with_front, with_back))
                        else:
                            front_item(i + 1, item, with_back)

                    def to_take(x):
                        if x[0] == "max":
                            max_group(b.plus(1), *x[1])
                        else:
                            banked(x)

                    for item in slot_items(0, with_front, with_back):
                        banked(item)
                    for h in range(NH):
                        taken = slot_order(h + 1, with_front, with_back)
                        early = (len(taken) + 1) // 2 if all(x[0] == "max" for x in taken) else 0
                        for own, n in mixed(TPB, early):
                            if own:
                                scores(b, h, n)
                            else:
                                to_take(taken[n])
                        for own, n in mixed(TPB if h else 0, len(taken) - early):
                            if own:
                                weighted(i, h - 1, n)
                            else:
                                to_take(taken[n + early])
                    weighted(i, NH - 1, 0)
                    if more:
                        turn_maxima(i + 1)
                    for kt in range(1, TPB):
                        weighted(i, NH - 1, kt)
                    for item in slot_items(NH + 1, with_front, with_back):
                        banked(item)

                pairs_loop(nc, pe, BATCH, turn)
                wait_taken(pe, BATCH - 2, BACK[-1])
                for item in BACK:
                    if before(item, False, True):
                        wait_taken(pe, BATCH - 1, before(item, False, True))
                    back_item(BATCH - 1, item, bank_of(item))

            @block.scalar
            def _(act):
                def std_of(i):
                    act.wait_ge(var_ready, i + 1)
                    act.activation(std[:], varp[:], ACT.Sqrt).then_inc(std_ready, 1)

                def take(i, item):
                    name, c = item
                    if name in ("q", "k"):
                        wait_ready(act, i, item)
                        col = (CC if name == "k" else 0) + c
                        act.activation((qT_hi if name == "q" else kT_hi)[:, c, :], bank_of(item)[:], ACT.Identity,
                                       bias=cols[:, col:col + 1]).then_inc(qk_hi_ready, 1)
                    if name == "qk":
                        own, before_ = turns_of(c)
                        need(act, stack_in[before_], 16 * 12 * (i + (CHUNKS.index(c) >= 2)))
                        act.wait_ge(rotk_ready, HC * i + CHUNKS.index(c) + 1)
                        act.activation(parts[own][:, K_HI, :], rotk[:], ACT.Copy).then_inc(hi_ready, 1)
                        wait_ready(act, i, item)
                        act.activation(parts[own][:, Q_HI, :], bank_of(item)[:], ACT.Identity, bias=cols[:, 8:9])\
                           .then_inc(hi_ready, 1)
                    if name not in BY_SCALAR:
                        return
                    wait_ready(act, i, item)
                    w = bank_of(item)
                    if name == "xT":
                        act.activation(xT[:, c, :], w[:], ACT.Copy).then_inc(front_act, 1)
                    else:
                        act.activation(yT[:, c, :], w[:], ACT.Copy).then_inc(back_act, 1)

                def exps(i, h):
                    x = NH * i + h
                    need(act, pv_ready, x - 1)
                    for j, width in ((0, BLK), (1, BLK - P), (2, BLK - P)):
                        act.wait_ge(score_ready, 3 * x + j + 1)
                        act.activation(prob[h % 2][:, PO[j]:PO[j] + width], score[j][:, 0:width], ACT.Exp,
                                       scale=scale).then_inc(exp_ready, 1)

                def o_take(i, c):
                    act.wait_ge(pv_ready, NH * i + 4 * c + 4)
                    if c == 0:
                        need(act, back_ready, len(BACK) * (i - 1) + HC)
                    act.activation(o_sb[:, c, :], obank[:], ACT.Copy).then_inc(o_out, 1)

                std_of(0)
                act.wait_ge(const_in, 16 * (N_CONST + 1))
                for item in front:
                    take(0, item)
                    if item == ("k", CC - 1):
                        std_of(1)

                def turn(b, more):
                    i = b.i

                    def banked(k):
                        for item in slot_items(k, more > 0, not isinstance(i, int) or i > 0):
                            take(i - 1 if item in BACK else i + 1, item)

                    banked(0)
                    for h in range(NH):
                        if h % 4 == 1 and h > 4:
                            o_take(i, h // 4 - 1)
                        exps(i, h)
                        banked(h + 1)
                        if h == 3 and more >= 2:
                            std_of(i + 2)
                    o_take(i, HC - 1)
                    banked(NH + 1)

                pairs_loop(nc, act, BATCH, turn)
                for item in BACK:
                    take(BATCH - 1, item)

            @block.gpsimd
            def _(pool):
                st = Steps(pool, held)

                def ln_apply(i):
                    pool.wait_ge(rstd_ready, i + 1)
                    need(pool, front_act, (i - 1) * NFA + 2)
                    st.settle()
                    st.step(pool.tensor_tensor(cell[:, 0:1], cell[:, 1:2], cell[:, 2:3], ALU.add))
                    for t in range(TPB):
                        last = pool.tensor_scalar(xln[:, t, :], xin[:, t, :], mv[:, t, 0:1],
                                                  rstd[:, t:t + 1], ALU.subtract, ALU.mult)
                    last.then_inc(ln_ready, 1)

                def between(i, item):
                    name, c = item
                    n = CHUNKS.index(c) if name in ("latq_s", "latk_s", "qk") else None
                    if name == "latq_s":
                        wait_taken(pool, i, item)
                        if n:
                            wait_ready(pool, i, ("qk", CHUNKS[n - 1]))
                        else:
                            need(pool, front_ready, len(front) * (i - 1) + front.index(("qk", CHUNKS[-1])) + 1)
                        pool.tensor_tensor(rotq[:], rot["latq"][:], rot["latq_s"][:], ALU.add).then_inc(rotq_ready, 1)
                    elif name == "latk_s":
                        wait_taken(pool, i, item)
                        need(pool, split_ready, HC * i + n)
                        pool.tensor_tensor(rotk[:], rot["latk"][:], rot["latk_s"][:], ALU.add).then_inc(rotk_ready, 1)
                    elif name == "qk":
                        p_ = parts[turns_of(c)[0]]
                        wait_taken(pool, i, item)
                        pool.tensor_tensor(p_[:, K_LO, :], rotk[:], p_[:, K_HI, :].bitcast(F32), ALU.subtract)\
                            .then_inc(split_ready, 1)

                def turn(b, more):
                    for k in range(len(SLOTS)):
                        if more:
                            for item in slot_items(k, True, False):
                                between(b.i + 1, item)
                        if k == 5 and more >= 2:
                            ln_apply(b.i + 2)
                    pool.wait_ge(xres_in, 16 * (b.i + 1))
                    pool.tensor_tensor(xres[:], xres[:], pbias[:].unsqueeze(1).to_broadcast([P, TPB, C]), ALU.add)\
                        .then_inc(xres_ready, 1)

                st.step(pool.memset(cell[:], 0.0))
                st.step(pool.memset(v[:], 0.0))
                for x in stacks3:
                    st.settle()
                    st.step(pool.memset(x[STACK:SHIFT, :, 0, :].bitcast(F32), 1.0))
                st.settle()
                st.step(pool.memset(v[:, :, :, HD:HD + 1], 1.0))
                ln_apply(0)
                for item in front:
                    between(0, item)
                    if item == ("qk", CHUNKS[0]):
                        ln_apply(1)
                pool.wait_ge(const_in, 16 * (N_CONST + 1))
                pairs_loop(nc, pool, BATCH, turn, st)

            @block.vector
            def _(dve):
                st = Steps(dve, vec)

                def ln_stats(i):
                    dve.wait_ge(x_in, 16 * (i + 1))
                    for t in range(TPB):
                        st.step(dve.bn_stats(stats[:, t, :], xin[:, t, :]))
                    need(dve, ln_ready, i)
                    st.settle_on(unused[:])
                    for t in range(TPB):
                        st.step(dve.bn_aggr(mv[:, t, :], stats[:, t, :]))
                    st.settle()
                    need(dve, std_ready, i)
                    dve.tensor_scalar(varp[:], mv[:, :, 1], EPS, None, ALU.add).then_inc(var_ready, 1)

                def ln_scale(i):
                    dve.wait_ge(std_ready, i + 1)
                    rsqrt_refined(dve, st, rstd, varp, std, newton)
                    dve.memset(unused[:], 0.0).then_inc(rstd_ready, 1)

                def take(i, item):
                    name, c = item
                    if name in BY_SCALAR:
                        return
                    wait_ready(dve, i, item)
                    w = bank_of(item)
                    if name == "v":
                        if c == 0:
                            need(dve, pv_ready, NH * i)
                        dve.tensor_tensor(v[:, 2 * c:2 * c + 2, :, 0:HD],
                                          w[:].rearrange("p (t h d) -> p t h d", t=2, h=NH),
                                          vbias[:].rearrange("p (h d) -> p h d", h=NH).unsqueeze(1)
                                          .to_broadcast([P, 2, NH, HD]), ALU.add).then_inc(front_dve, 1)
                    elif name == "o":
                        heads = w[:].rearrange("p (t h l) -> p t h l", t=TPB, h=4)
                        need(dve, back_dve, NBD * i + c)
                        st.step(dve.reciprocal(orec[:], heads[:, :, :, HD]))
                        st.settle()
                        dve.tensor_tensor(ytok[:, :, c * 64:(c + 1) * 64].rearrange("p t (h d) -> p t h d", h=4),
                                          heads[:, :, :, 0:HD], orec[:].unsqueeze(3).to_broadcast([P, TPB, 4, HD]),
                                          ALU.mult).then_inc(back_dve, 1)
                    elif name == "proj":
                        if c == 0:
                            dve.wait_ge(xres_ready, i + 1)
                        dve.tensor_tensor(xres[:, 2 * c:2 * c + 2, :], w[:].rearrange("p (t n) -> p t n", t=2),
                                          xres[:, 2 * c:2 * c + 2, :], ALU.add).then_inc(back_dve, 1)
                    elif name in ("q", "k"):
                        n = (CC if name == "k" else 0) + c
                        hi, lo = (qT_hi, qT_lo) if name == "q" else (kT_hi, kT_lo)
                        dve.wait_ge(qk_hi_ready, 2 * CC * i + n + 1)
                        dve.scalar_tensor_tensor(lo[:, c, :], w[:], cols[:, n:n + 1], hi[:, c, :].bitcast(F32),
                                                 ALU.add, ALU.subtract).then_inc(front_dve, 1)
                    elif name == "qk":
                        p_ = parts[turns_of(c)[0]]
                        dve.wait_ge(hi_ready, 2 * (HC * i + CHUNKS.index(c)) + 2)
                        dve.scalar_tensor_tensor(p_[:, Q_LO, :], w[:], cols[:, 8:9], p_[:, Q_HI, :].bitcast(F32),
                                                 ALU.add, ALU.subtract).then_inc(front_dve, 1)
                    else:
                        is_q, swapped = name[3] == "q", name.endswith("_s")
                        bias = cols[:, (4 if is_q else 6) + swapped:(5 if is_q else 7) + swapped]
                        need(dve, rotq_ready if is_q else rotk_ready, HC * i + CHUNKS.index(c))
                        dve.scalar_tensor_tensor(rot[name][:], w[:], bias, sin[:] if swapped else cos[:],
                                                 ALU.add, ALU.mult).then_inc(front_dve, 1)

                def slot_takes(i_front, i_back, k, with_front, with_back):
                    for x in slot_order(k, with_front, with_back):
                        if x[0] == "max":
                            maxima(i_front, *x[1])
                        else:
                            take(i_back if x in BACK else i_front, x)

                def maxima(i, h, g):
                    dve.wait_ge(smax_ready, len(GROUPS) * (NH * i + MAX_AT[h]) + g + 1)
                    if MAX_AT[h] == 0 and g == 0:
                        need(dve, neg_ready, i)
                    for t, o in group_tiles(g):
                        last = dve.tensor_reduce(negmax[:, t, h:h + 1], smax_bank(h, g)[:, o:o + (t + 1) * P],
                                                 AX.X, ALU.max, negate=True)
                    last.then_inc(smax_read, 1)

                def split_maxima(i):
                    dve.wait_ge(neg_ready, i + 1)
                    need(dve, shift_in, 64 * i)
                    st.step(dve.tensor_copy(m_hi[:], smax[0][0:NH, :]))
                    st.settle()
                    dve.tensor_tensor(m_lo[:], smax[0][0:NH, :], m_hi[:].bitcast(F32), ALU.subtract)\
                       .then_inc(m_ready, 1)

                st.step(dve.memset(stacks[STACK:SHIFT, :, 0, :].bitcast(F32), 1.0))
                st.step(dve.memset(bvb[:], 0.0))
                st.step(dve.memset(kvbb[:], 0.0))
                ln_stats(0)
                ln_scale(0)
                dve.wait_ge(const_in, 16 * (N_CONST + 1))
                st.step(dve.tensor_copy(ident_b[:], ident[:]))
                st.step(dve.tensor_copy(masks[:], masks_f))
                st.step(dve.tensor_copy(latq_hi[:], latq_w))
                st.step(dve.tensor_copy(latk_hi[:], latk_w))
                st.settle()
                for g in range(2):
                    st.step(dve.tensor_scalar(bvb[:, g, :], bvb[:, g, :], bv[:, g:g + 1], None, ALU.add))
                st.step(dve.tensor_scalar(kvbb[:], kvbb[:], kvb[:], None, ALU.add))
                dve.wait_ge(set_mm, 1)
                st.settle()
                st.step(dve.tensor_tensor(latq_lo[:], latq_w, latq_hi[:].bitcast(F32), ALU.subtract))
                st.step(dve.tensor_tensor(latk_lo[:], latk_w, latk_hi[:].bitcast(F32), ALU.subtract))
                dve.tensor_tensor(at8[:], work[0][:, 0:P], bmask[:], ALU.mult).then_inc(set_up, 1)
                dve.wait_ge(set_mm, 2)
                st.step(dve.tensor_copy(wvp[:], work[1][:].rearrange("p (c n) -> p c n", c=CC)))
                dve.tensor_tensor(vbias[:], score[0][:, 0:C], l2ob[:], ALU.add).then_inc(set_up, 1)
                dve.wait_ge(set_up, 2)
                dve.wait_ge(held, 5)
                ln_stats(1)
                for k in range(len(SLOTS)):
                    slot_takes(0, None, k, True, False)
                    if k == 4:
                        ln_scale(1)
                split_maxima(0)

                def turn(b, more):
                    i = b.i
                    for k in range(len(SLOTS)):
                        if k == len(SLOTS) - 1 and more:
                            split_maxima(i + 1)
                        slot_takes(i + 1, i - 1, k, more > 0, not isinstance(i, int) or i > 0)
                        if k == 3 and more >= 2:
                            ln_stats(i + 2)
                        if k == 5 and more >= 2:
                            ln_scale(i + 2)

                pairs_loop(nc, dve, BATCH, turn, st)
                for item in BACK:
                    take(BATCH - 1, item)


def program(nc, a):
    def scratch(name, shape):
        return nc.dram_tensor(name, shape, F32, kind="Internal").ap()

    xtab = scratch("xtab", [TOK + P, ROW])
    cumtab = scratch("cumtab", [(NT + 1) * E, P])
    cend = scratch("cend", [E, NT])
    x1 = scratch("x1", [TOK + P, C])
    x2 = scratch("x2", [TOK, C])
    ffn_dense(nc, "d1", a["x"], x1, xtab, cumtab, cend, a)
    ffn_routed(nc, "r1", x1, xtab, cumtab, cend, a)
    attention(nc, "at", x1, x2, a)
    ffn_dense(nc, "d2", x2, a["out"], xtab, cumtab, cend, a)
    ffn_routed(nc, "r2", a["out"], xtab, cumtab, cend, a)


def laid_out(v):
    f = {k: np.asarray(x) for k, x in v.items()}

    def image(w):
        return np.ascontiguousarray(w.T.reshape(-1, P, w.shape[0]).transpose(1, 0, 2))

    part = np.arange(P)
    pair = np.arange(L) ^ 1
    m = {"x": np.ascontiguousarray(f["L0_attn_x"].reshape(TOK, C)), "wg": image(f["L0_ffn_wg"]),
         "sw1": image(f["L0_ffn_shared_w1"]), "sw2": image(f["L0_ffn_shared_w2"])}
    w1, w2 = f["L0_ffn_expert_w1"], f["L0_ffn_expert_w2"]
    m["experts"] = np.concatenate(
        [w1.transpose(0, 2, 1).reshape(E, CC, P, 2 * F).transpose(0, 2, 1, 3).reshape(E, P, CC * 2 * F),
         w2.transpose(0, 2, 1).reshape(E, FC, P, C).transpose(0, 2, 1, 3).reshape(E, P, FC * C)], 2)
    m["ident"] = np.eye(P, dtype=np.float32)
    tri = np.zeros((P, TPB, BLK), np.float32)
    for t in range(TPB):
        tri[:, t, :] = np.arange(BLK)[None, :] >= t * P + part[:, None]
    m["tri"] = tri
    m["slot"] = np.stack([part] * GRP + [P + part % TAIL, part], 1).astype(np.float32)
    first = GRP * np.arange(NG)
    m["erow"] = np.stack([np.broadcast_to(first + k, (P, NG)) for k in range(GRP)]
                         + [first[None] + part[:, None] // TAIL], 2).astype(np.float32)
    wa, ba = f["L0_attn_c_attn_w"], f["L0_attn_c_attn_b"]
    m["wqkin"] = image(wa[0:2 * C])
    for name, w in (("latq", f["L0_attn_q2l_w"]), ("latk", f["L0_attn_kv2l_w"])):
        lat = np.zeros((P, 2, 2, P), np.float32)
        for half in range(2):
            for h in range(4):
                rows = slice(64 * half + HD * h, 64 * half + HD * (h + 1))
                lat[rows, half, 0, L * h:L * (h + 1)] = w.T
                lat[rows, half, 1, L * h:L * (h + 1)] = w[pair].T
        m[name] = lat
    qkw = np.zeros((P, P), np.float32)
    for h in range(4):
        qkw[L * h:L * (h + 1), L * h:L * (h + 1)] = f["L0_attn_wqk_w"].T
    m["qkw"] = qkw
    qb, kb = f["L0_attn_q2l_b"], f["L0_attn_kv2l_b"]
    m["cols"] = np.stack([ba[0:P], ba[P:C], ba[C:C + P], ba[C + P:2 * C], np.tile(qb, 4), np.tile(qb[pair], 4),
                          np.tile(kb, 4), np.tile(kb[pair], 4), np.tile(f["L0_attn_wqk_b"], 4)], 1)
    inv = (1.0 / 10000.0 ** (np.arange(0, L, 2, dtype=np.float32) / np.float32(L))).astype(np.float32)
    freqs = np.outer(np.arange(SEQ, dtype=np.float32), inv).astype(np.float32)
    sign = np.where(np.arange(L) % 2 == 0, -1.0, 1.0).astype(np.float32)
    m["cos"] = np.tile(np.repeat(np.cos(freqs), 2, axis=1).T, (4, 1)).astype(np.float32)
    m["sin"] = np.tile(np.repeat(np.sin(freqs), 2, axis=1).T * sign[:, None], (4, 1)).astype(np.float32)
    m["kv8"] = np.tile(f["L0_attn_kv2l_w"], (1, 8))
    m["l2o8"] = np.tile(f["L0_attn_l2o_w"].T, (1, 8))
    m["bmask"] = (part[:, None] // HD == part[None] // HD).astype(np.float32)
    m["wv"] = np.ascontiguousarray(wa[2 * C:].reshape(2, P, C).transpose(1, 0, 2))
    m["bv"] = np.ascontiguousarray(ba[2 * C:].reshape(2, P).T)
    m["kvb"] = np.ascontiguousarray(kb[:, None])
    m["l2ob"] = np.tile(f["L0_attn_l2o_b"], NH)
    m["wp"] = image(f["L0_attn_cproj_w"])
    m["pbias"] = f["L0_attn_cproj_b"]
    hidden = np.where(part[None] > part[:, None], -1.0e30, 0.0)
    m["masks"] = np.stack([hidden, hidden.T], 1).astype(np.float32)
    return {k: np.ascontiguousarray(x) for k, x in m.items()}


def kernel(**inputs):
    import concourse.bacc as bacc
    from concourse.bass_utils import run_bass_kernel_spmd

    arrays = laid_out(inputs)
    nc = bacc.Bacc("TRN2", target_bir_lowering=False, num_devices=1)
    args = {k: nc.dram_tensor(f"in_{k}", x.shape, F32, kind="ExternalInput").ap() for k, x in arrays.items()}
    args["out"] = nc.dram_tensor("out_0", (TOK + P, C), F32, kind="ExternalOutput").ap()
    program(nc, args)
    r = run_bass_kernel_spmd(nc, [{f"in_{k}": x for k, x in arrays.items()}], core_ids=[0])
    return r.results[0]["out_0"][0:TOK].reshape(BATCH, SEQ, C)
```
